# Optimizing a Trainium2 kernel written in Bass

```python
import numpy as np
import jax
import jax.numpy as jnp

def _softmax(x, axis=-1):
    return jax.nn.softmax(x, axis=axis)

def _gelu(x):
    return jax.nn.gelu(x, approximate=True)

def _silu(x):
    return jax.nn.silu(x)

def _sigmoid(x):
    return jax.nn.sigmoid(x)

def _layernorm(x, axis=-1, eps=1e-05):
    m = jnp.mean(x, axis=axis, keepdims=True)
    v = jnp.var(x, axis=axis, keepdims=True)
    return (x - m) / jnp.sqrt(v + eps)

def _scatter_add(tgt, idx, src, axis=0):
    return tgt.at[idx].add(src)

def _segment_sum(src, seg, n):
    return jax.ops.segment_sum(src, seg, n)
kernel_name = 'mk_adaln_ffn_d1_seqx_r4_c89a0a'

def setup_inputs(seed: int=0):
    np.random.seed(seed)
    _w = jnp.asarray

    def _rec_inputs():
        import jax
        import jax.numpy as jnp
        _rk = jax.random.key(seed)
        x = 7.22e-05 + 1 * jax.random.normal(jax.random.fold_in(_rk, 1), (16, 256, 512), jnp.float32)
        _lenS = 256 - jax.random.randint(jax.random.fold_in(_rk, 7), (16,), 0, max(1, 256 // 4) + 1, jnp.int32)
        _lenS2 = 256 - jax.random.randint(jax.random.fold_in(_rk, 8), (16,), 0, max(1, 256 // 4) + 1, jnp.int32)
        cond_2048 = jax.random.bernoulli(jax.random.fold_in(_rk, 11), 0.5063, (16, 512)).astype(jnp.float32)
        return (x, cond_2048)
    x, cond_2048 = _rec_inputs()

    def _L0_cond_setup():
        import jax, jax.numpy as jnp
        import numpy as np
        NH = 8
        NEG = -1e+30
        key = jax.random.key(seed)
        k1, k2, k3, k4 = jax.random.split(key, 4)
        B, D, T = (4, 256, 512)
        x = jax.random.normal(k1, (B, D, T), dtype=jnp.float32)
        mask = jax.random.randint(k2, (B, T), 0, 2).astype(jnp.float32)
        lim = float(np.sqrt(6.0 / (D + D)))
        Wq = jax.random.uniform(k3, (D, D), dtype=jnp.float32, minval=-lim, maxval=lim)
        Wo = jax.random.uniform(k4, (D, D), dtype=jnp.float32, minval=-lim, maxval=lim)
        return {'x': x, 'mask': mask, 'Wq': Wq, 'Wo': Wo}
    _L0_cond_all = _L0_cond_setup()
    _L0_cond_in = {k: v for k, v in _L0_cond_all.items() if k in ('Wq', 'Wo')}
    del _L0_cond_all

    def _L0_ffn_setup():
        import jax, jax.numpy as jnp
        import numpy as np
        B, S, D, I, E, K = (4, 256, 512, 256, 8, 2)
        key = jax.random.key(seed)
        ks = jax.random.split(key, 7)

        def w(k, shape, fan_in):
            return jax.random.normal(k, shape, dtype=jnp.float32) * fan_in ** (-0.5)
        return {'hidden_states': jax.random.normal(ks[0], (B, S, D), dtype=jnp.float32), 'router_w': w(ks[1], (D, E), D), 'gate_up_w': w(ks[2], (E, D, 2 * I), D), 'down_w': w(ks[3], (E, I, D), I), 'shared_gate_w': w(ks[4], (D, I), D), 'shared_up_w': w(ks[5], (D, I), D), 'shared_down_w': w(ks[6], (I, D), I)}
    _L0_ffn_all = _L0_ffn_setup()
    _L0_ffn_in = {k: v for k, v in _L0_ffn_all.items() if k in ('router_w', 'gate_up_w', 'down_w', 'shared_gate_w', 'shared_up_w', 'shared_down_w')}
    del _L0_ffn_all
    return {'x': x, 'cond_2048': cond_2048, 'L0_cond_Wq': _L0_cond_in['Wq'], 'L0_cond_Wo': _L0_cond_in['Wo'], 'L0_ffn_router_w': _L0_ffn_in['router_w'], 'L0_ffn_gate_up_w': _L0_ffn_in['gate_up_w'], 'L0_ffn_down_w': _L0_ffn_in['down_w'], 'L0_ffn_shared_gate_w': _L0_ffn_in['shared_gate_w'], 'L0_ffn_shared_up_w': _L0_ffn_in['shared_up_w'], 'L0_ffn_shared_down_w': _L0_ffn_in['shared_down_w']}

def reference(x, cond_2048, L0_cond_Wq, L0_cond_Wo, L0_ffn_router_w, L0_ffn_gate_up_w, L0_ffn_down_w, L0_ffn_shared_gate_w, L0_ffn_shared_up_w, L0_ffn_shared_down_w):
    import jax
    import jax.numpy as jnp

    def _L0_cond_ref(x, mask, Wq, Wo):
        import jax, jax.numpy as jnp
        import numpy as np
        NH = 8
        NEG = -1e+30
        B, D, T = x.shape
        dk = D // NH
        scale = 1.0 / jnp.sqrt(jnp.asarray(dk, x.dtype))
        xt = jnp.transpose(x, (0, 2, 1))
        q = xt @ Wq.T
        qh = q.reshape(B, T, NH, dk).transpose(0, 2, 1, 3)
        scores = scale * jnp.einsum('bhqd,bhkd->bhqk', qh, qh)
        cmask = mask[:, None, None, :]
        rmask = mask[:, None, :, None]
        logits = (scores * cmask + (1.0 - cmask) * NEG) * rmask
        attn = jax.nn.softmax(logits, axis=-1)
        ctx = jnp.einsum('bhqk,bhkd->bhqd', attn, qh)
        ctx = ctx.transpose(0, 2, 1, 3).reshape(B, T, D)
        out = ctx @ Wo.T
        return jnp.transpose(out, (0, 2, 1))

    def _L0_ffn_ref(hidden_states, router_w, gate_up_w, down_w, shared_gate_w, shared_up_w, shared_down_w):
        import jax, jax.numpy as jnp
        import numpy as np
        B, S, D, I, E, K = (4, 256, 512, 256, 8, 2)
        Bb, Ss, Dd = hidden_states.shape
        x = hidden_states.reshape(-1, Dd)
        T = x.shape[0]
        shared = jax.nn.silu(x @ shared_gate_w) * (x @ shared_up_w) @ shared_down_w
        logits = x @ router_w
        top_val, top_idx = jax.lax.top_k(logits, K)
        probs = jnp.zeros_like(logits).at[jnp.arange(T)[:, None], top_idx].set(jax.nn.sigmoid(top_val))
        xin = probs.T[:, :, None] * x[None]
        gu = jnp.einsum('etd,edf->etf', xin, gate_up_w)
        gate, up = jnp.split(gu, 2, axis=-1)
        h = jax.nn.silu(gate) * up
        expert_out = jnp.einsum('eti,eid->etd', h, down_w)
        combined = shared + expert_out.sum(axis=0)
        return combined.reshape(Bb, Ss, Dd)
    x = x + _L0_ffn_ref(_L0_cond_ref(x, cond_2048, L0_cond_Wq, L0_cond_Wo), L0_ffn_router_w, L0_ffn_gate_up_w, L0_ffn_down_w, L0_ffn_shared_gate_w, L0_ffn_shared_up_w, L0_ffn_shared_down_w)
    return x

_drawn_inputs = setup_inputs


def setup_inputs(seed=0):
    import zlib

    import numpy as np

    out = dict(_drawn_inputs(seed))
    spreads = {}
    factors = {}
    for name, (base, spread) in spreads.items():
        noise = np.random.default_rng([zlib.crc32(name.encode()), seed]).standard_normal(out[name].shape)
        drawn = base * np.exp(spread * noise) if base else spread * noise
        out[name] = jnp.asarray(drawn.astype(out[name].dtype))
    for name, factor in factors.items():
        out[name] = (out[name] * factor).astype(out[name].dtype)
    return out
```

```python
from contextlib import ExitStack

import concourse.bass as bass
from concourse import mybir

ALU = mybir.AluOpType
ACT = mybir.ActivationFunctionType
AX = mybir.AxisListType
F32 = mybir.dt.float32
I32 = mybir.dt.int32

P = 128
BANK = 512
DK = 32
HEADS_AT_ONCE = P // DK
NEG = -1e30
LOWEST = -3.0e38

FIRST, MIDDLE, LAST = range(3)
MISC = [("q1", 0, "A"), ("prev_recip1", 1, "B"), ("v1", 2, "A"), ("prev_hid0", 3, "A"), ("prev_hid1", 3, "B"),
        ("next_q0", 4, "A"), ("prev_hidT0", 4, "B"), ("prev_hidT1", 5, "A"), ("recip0", 5, "B"),
        ("next_v0", 6, "A"), ("prev_router", 6, "B")]
MISC_SETUP = 5


def misc_list(kind):
    return [m for m in MISC
            if not (kind == FIRST and m[0].startswith("prev")) and not (kind == LAST and m[0].startswith("next"))]


def misc_count(b, kind, name):
    names = [m[0] for m in misc_list(kind)]
    before = MISC_SETUP if kind == FIRST else MISC_SETUP + len(misc_list(FIRST)) + len(misc_list(MIDDLE)) * (b - 1)
    return before + names.index(name)


def build(nc, x, cond, wq, wo, router_w, gate_up_w, down_w, sh_gate_w, sh_up_w, sh_down_w, out, stop_after=9):
    B, D, T = x.shape
    E, _, F2 = gate_up_w.shape
    I = F2 // 2
    KD = D // P
    KT = T // P
    NQ = T // P
    G = D // P
    STEPS = G * NQ
    TOKENS = B * D
    TT = TOKENS // P
    SCALE = float(DK) ** -0.5
    LOGIT_NEG = NEG / SCALE
    assert T == BANK and KD == G == 2 and STEPS == 8

    ctx = ExitStack()
    with ctx:
        def sb(name, shape, dt=F32):
            return ctx.enter_context(nc.sbuf_tensor(name, shape, dt))

        def sem(name):
            return ctx.enter_context(nc.semaphore(name))

        bank = [ctx.enter_context(nc.psum_tensor(f"bank{i}", [P, BANK], F32)) for i in range(8)]
        logit_bank = bank[0:4]
        turn_bank = bank[4:6]
        ctx_bank = bank[6]
        misc = bank[7]

        hidden = nc.dram_tensor("hidden_dram", [TOKENS, T], F32)

        x_all = sb("x_all", [P, B * KD, T])
        ident = sb("ident", [P, P])
        logits_all = sb("logits_all", [P, TT, E])
        shared_in = [sb(f"shared_in{i}", [P, KT, I]) for i in range(2)]
        shared_out = sb("shared_out", [P, I // P, T])
        shared_loaded = sem("shared_loaded")

        attention = ExitStack()
        ctx.enter_context(attention)

        def sb(name, shape, dt=F32):
            return attention.enter_context(nc.sbuf_tensor(name, shape, dt))

        w_nat = sb("w_nat", [P, 2, KD, D])
        wqT = sb("wqT", [P, KD, D])
        woT = sb("woT", [P, KD, D])
        mask_nat = sb("mask_nat", [B * NQ, P])
        row_scale = sb("row_scale", [P, B * NQ])
        router_sb = sb("router_sb", [P, KT, E])
        mask_row = [sb(f"mask_row{g}", [P, T]) for g in range(G)]
        neg_row = [sb(f"neg_row{g}", [P, T]) for g in range(G)]
        unit_scale = [sb(f"unit_scale{g}", [P, NQ]) for g in range(G)]
        qT = [sb(f"qT{g}", [P, T]) for g in range(G)]
        qTm = [sb(f"qTm{g}", [P, T]) for g in range(G)]
        vals = [sb(f"vals{g}", [P, NQ, P]) for g in range(G)]
        logit = [sb(f"logit{i}", [P, 4, T]) for i in range(2)]
        probs = [sb(f"probs{i}", [P, 4, T]) for i in range(2)]
        probsT = [sb(f"probsT{i}", [P, 4, NQ, P]) for i in range(2)]
        row_max = sb("row_max", [P, 2, 4])
        neg_max = sb("neg_max", [P, 2, 4])
        row_sum = sb("row_sum", [P, G, NQ, 4])
        inv_sum = sb("inv_sum", [P, NQ * 4, DK])
        inv_cols = sb("inv_cols", [P, T])
        ctxn = sb("ctxn", [P, G, T])
        hid = sb("hid", [P, KD, T])
        hidT = sb("hidT", [P, KD, KT, P])

        x_loaded = sem("x_loaded")
        wq_loaded = sem("wq_loaded")
        wo_loaded = sem("wo_loaded")
        mask_loaded = sem("mask_loaded")
        router_loaded = sem("router_loaded")
        mask_row_loaded = [sem(f"mask_row_loaded{g}") for g in range(G)]
        ident_cleared = sem("ident_cleared")
        ident_ready = sem("ident_ready")
        misc_written = sem("misc_written")
        misc_emptied = sem("misc_emptied")
        unit_prepared = sem("unit_prepared")
        logits_written = sem("logits_written")
        logits_read = sem("logits_read")
        neg_max_ready = sem("neg_max_ready")
        probs_ready = sem("probs_ready")
        probs_turned = sem("probs_turned")
        even_copied = sem("even_copied")
        odd_copied = sem("odd_copied")
        step_summed = sem("step_summed")
        inv_ready = sem("inv_ready")
        ctx_ready = sem("ctx_ready")
        hidden_stored = sem("hidden_stored")
        waits_passed = sem("waits_passed")
        pool_waits_passed = sem("pool_waits_passed")

        block = attention.enter_context(nc.Block())

        def rows(eng, body):
            body(0, FIRST)
            with eng.Fori(1, B - 1) as b:
                body(b, MIDDLE)
            body(B - 1, LAST)

        def has(kind, name):
            return name in [m[0] for m in misc_list(kind)]

        def misc_last():
            return misc_count(B - 1, LAST, misc_list(LAST)[-1][0]) + 1

        @block.sync
        def _(sp):
            sp.sem_inc(hidden_stored, 16)
            sp.dma_start(w_nat[:, 0, :, :], wq.rearrange("(m p) d -> p m d", p=P)).then_inc(wq_loaded, 16)
            sp.dma_start(mask_nat[:, :], cond.rearrange("b (q p) -> (b q) p", p=P)).then_inc(mask_loaded, 16)
            sp.dma_start(mask_row[0][:, :], cond[0:1, :].partition_broadcast(P)).then_inc(mask_row_loaded[0], 16)
            sp.dma_start(x_all[:, 0:KD, :], x[0].rearrange("(k p) t -> p k t", p=P)).then_inc(x_loaded, 16)
            sp.dma_start(w_nat[:, 1, :, :], wo.rearrange("(m p) d -> p m d", p=P)).then_inc(wo_loaded, 16)
            sp.dma_start(router_sb[:, :, :], router_w.rearrange("(k p) e -> p k e", p=P)).then_inc(router_loaded, 16)

            def store_hidden(b, copied):
                sp.wait_ge(misc_emptied, copied)
                sp.dma_start(hidden[bass.ds(b * D, D), :].rearrange("(k p) t -> p k t", p=P), hid[:, :, :])\
                    .then_inc(hidden_stored, 16)

            def body(b, kind):
                if kind != FIRST:
                    sp.wait_ge(unit_prepared, 2 * b)
                sp.dma_start(mask_row[1][:, :], cond[bass.ds(b, 1), :].partition_broadcast(P))\
                    .then_inc(mask_row_loaded[1], 16)
                if kind != LAST:
                    sp.wait_ge(x_loaded, 16 * (b + 1))
                    sp.dma_start(x_all[:, bass.ds((b + 1) * KD, KD), :],
                                 x[bass.ds(b + 1, 1)].rearrange("o (k p) t -> p (o k) t", p=P))\
                        .then_inc(x_loaded, 16)
                    sp.wait_ge(unit_prepared, 2 * b + 1)
                    sp.dma_start(mask_row[0][:, :], cond[bass.ds(b + 1, 1), :].partition_broadcast(P))\
                        .then_inc(mask_row_loaded[0], 16)
                if kind != FIRST:
                    store_hidden(b - 1, misc_count(b, kind, "prev_hid1") + 1)

            for dst, src in zip(shared_in, (sh_gate_w, sh_up_w)):
                sp.dma_start(dst[:, :, :], src.rearrange("(k p) i -> p k i", p=P)).then_inc(shared_loaded, 16)
            sp.dma_start(shared_out[:, :, :], sh_down_w.rearrange("(k p) d -> p k d", p=P)).then_inc(shared_loaded, 16)
            rows(sp, body)
            store_hidden(B - 1, misc_last() + 3)
            sp.wait_ge(hidden_stored, 16 * B + 16)

        @block.gpsimd
        def _(pool):
            nc.gpsimd.memset(ident[:, :], 0.0).then_inc(ident_cleared, 1)
            pool.wait_ge(ident_cleared, 1)
            nc.gpsimd.affine_select(out=ident[:, :], in_=ident[:, :], compare_op=ALU.not_equal, fill=1.0,
                                    base=0, pattern=[[-1, P]], channel_multiplier=1).then_inc(ident_ready, 1)

            def prepare(b, g, loads, q_in_sbuf, steps_before):
                pool.wait_ge(misc_emptied, 3)
                pool.wait_ge(mask_row_loaded[g], 16 * loads)
                if steps_before is not None:
                    pool.wait_ge(probs_ready, 4 * steps_before)
                pool.sem_inc(pool_waits_passed, 1)
                nc.gpsimd.tensor_scalar(neg_row[g][:, :], mask_row[g][:, :], -LOGIT_NEG, LOGIT_NEG, ALU.mult, ALU.add)
                nc.gpsimd.tensor_copy(unit_scale[g][:, :], row_scale[:, bass.ds(b * NQ, NQ)])
                pool.wait_ge(misc_emptied, q_in_sbuf)
                nc.gpsimd.tensor_tensor(qTm[g][:, :], qT[g][:, :], mask_row[g][:, :], ALU.mult)\
                    .then_inc(unit_prepared, 1)

            prepare(0, 0, 1, 4, None)

            def body(b, kind):
                prepare(b, 1, b + 1, misc_count(b, kind, "q1") + 1, None if kind == FIRST else STEPS * b)
                if kind != LAST:
                    prepare(b + 1, 0, b + 2, misc_count(b, kind, "next_q0") + 1, STEPS * b + NQ)

            rows(pool, body)

        @block.tensor
        def _(pe):
            def turn(dst, src, n=P):
                return nc.tensor.transpose(dst, src, ident[0:n, 0:n])

            def project_q(b, g):
                for k in range(KD):
                    last = nc.tensor.matmul(misc[:, :], wqT[:, k, g * P:(g + 1) * P],
                                            x_all[:, b * KD + k, :] if isinstance(b, int)
                                            else x_all[:, bass.ds(b * KD + k, 1), :].rearrange("p o t -> p (o t)"),
                                            start=(k == 0), stop=(k == KD - 1))
                last.then_inc(misc_written, 1)

            def values(g):
                for k in range(NQ):
                    last = turn(misc[:, k * P:(k + 1) * P], qT[g][:, k * P:(k + 1) * P])
                last.then_inc(misc_written, 1)

            def recips(u, g):
                pe.wait_ge(inv_ready, u + 1)
                for q in range(NQ):
                    last = turn(misc[:, q * P:(q + 1) * P],
                                inv_sum[:, q * 4:(q + 1) * 4, :].rearrange("p h d -> p (h d)"))
                last.then_inc(misc_written, 1)

            def hidden_half(b, e):
                if e == 0:
                    pe.wait_ge(ctx_ready, 2 * b + 2)
                for g in range(G):
                    last = nc.tensor.matmul(misc[:, :], woT[:, g, e * P:(e + 1) * P], ctxn[:, g, :],
                                            start=(g == 0), stop=(g == G - 1))
                last.then_inc(misc_written, 1)

            def hidden_turn(e):
                for k in range(KT):
                    last = turn(misc[:, k * P:(k + 1) * P], hid[:, e, k * P:(k + 1) * P])
                last.then_inc(misc_written, 1)

            def route():
                for e in range(KD):
                    for k in range(KT):
                        last = nc.tensor.matmul(misc[:, e * E:(e + 1) * E], hidT[:, e, k, :], router_sb[:, k, :],
                                                start=(k == 0), stop=(k == KT - 1))
                last.then_inc(misc_written, 1)

            def use_misc(b, kind, slot, place):
                for name, s, a in misc_list(kind):
                    if (s, a) != (slot, place):
                        continue
                    pe.wait_ge(misc_emptied, misc_count(b, kind, name))
                    if name == "q1":
                        pe.wait_ge(x_loaded, 16 * (b + 1))
                        project_q(b, 1)
                    elif name == "next_q0":
                        pe.wait_ge(x_loaded, 16 * (b + 2))
                        project_q(b + 1, 0)
                    elif name == "v1":
                        values(1)
                    elif name == "next_v0":
                        values(0)
                    elif name == "prev_recip1":
                        recips(2 * b - 1, 1)
                    elif name == "recip0":
                        recips(2 * b, 0)
                    elif name == "prev_hid0":
                        hidden_half(b - 1, 0)
                    elif name == "prev_hid1":
                        hidden_half(b - 1, 1)
                    elif name == "prev_hidT0":
                        hidden_turn(0)
                    elif name == "prev_hidT1":
                        hidden_turn(1)
                    elif name == "prev_router":
                        route()

            def logits(n, g, q):
                for h in range(4):
                    r = slice(h * DK, (h + 1) * DK)
                    nc.tensor.matmul(logit_bank[h][:, :], qT[g][r, q * P:(q + 1) * P], qTm[g][r, :],
                                     start=True, stop=True).then_inc(logits_written, 1)

            def turn_probs(m, i, h):
                pe.wait_ge(probs_ready, 4 * m + h + 1)
                copied = even_copied if h % 2 == 0 else odd_copied
                if not (isinstance(m, int) and 2 * m + h // 2 == 0):
                    pe.wait_ge(copied, 2 * m + h // 2)
                for k in range(NQ):
                    last = turn(turn_bank[h % 2][:, k * P:(k + 1) * P], probs[i][:, h, k * P:(k + 1) * P])
                last.then_inc(probs_turned, 1)

            def weigh(m, i, g, q, u):
                pe.wait_ge(even_copied, 2 * m + 2)
                pe.wait_ge(odd_copied, 2 * m + 2)
                if q == 0 and not (isinstance(u, int) and u == 0):
                    pe.wait_ge(ctx_ready, u)
                for k in range(NQ):
                    for h in range(4):
                        r = slice(h * DK, (h + 1) * DK)
                        last = nc.tensor.matmul(ctx_bank[r, q * P:(q + 1) * P], vals[g][:, k, r],
                                                probsT[i][:, h, k, :], start=(k == 0), stop=(k == NQ - 1))
                last.then_inc(step_summed, 1)

            pe.wait_ge(ident_ready, 1)
            for i, loaded in enumerate((wq_loaded, wo_loaded)):
                pe.wait_ge(loaded, 16)
                if i:
                    pe.wait_ge(misc_emptied, i)
                for k in range(KD):
                    for m in range(KD):
                        c = k * D + m * P
                        last = turn(misc[:, c:c + P], w_nat[:, i, m, k * P:(k + 1) * P])
                last.then_inc(misc_written, 1)
            pe.wait_ge(misc_emptied, 2)
            pe.wait_ge(mask_loaded, 16)
            turn(misc[:, 0:B * NQ], mask_nat[:, :], B * NQ).then_inc(misc_written, 1)
            pe.wait_ge(misc_emptied, 3)
            pe.wait_ge(x_loaded, 16)
            project_q(0, 0)
            pe.wait_ge(misc_emptied, 4)
            values(0)
            pe.wait_ge(router_loaded, 16)

            def body(b, kind):
                for s in range(STEPS):
                    g, q = divmod(s, NQ)
                    n = STEPS * b + s
                    some = kind != FIRST
                    if some or s >= 1:
                        turn_probs(n - 1, (s - 1) % 2, 0)
                        turn_probs(n - 1, (s - 1) % 2, 1)
                        pe.wait_ge(logits_read, 4 * n)
                    if q == 0:
                        pe.wait_ge(unit_prepared, 2 * b + g + 1)
                    logits(n, g, q)
                    use_misc(b, kind, s, "A")
                    if some or s >= 1:
                        turn_probs(n - 1, (s - 1) % 2, 2)
                        turn_probs(n - 1, (s - 1) % 2, 3)
                    if some or s >= 2:
                        g2, q2 = divmod((s - 2) % STEPS, NQ)
                        u2 = 2 * b + g2 if s >= 2 else 2 * b - 1
                        weigh(n - 2, s % 2, g2, q2, u2)
                    use_misc(b, kind, s, "B")

            rows(pe, body)
            n = STEPS * B
            for h in range(4):
                turn_probs(n - 1, (STEPS - 1) % 2, h)
            weigh(n - 2, 0, 1, NQ - 2, 2 * B - 1)
            weigh(n - 1, 1, 1, NQ - 1, 2 * B - 1)
            m = misc_last()
            for i, f in enumerate((lambda: recips(2 * B - 1, 1), lambda: hidden_half(B - 1, 0),
                                   lambda: hidden_half(B - 1, 1), lambda: hidden_turn(0),
                                   lambda: hidden_turn(1), route)):
                pe.wait_ge(misc_emptied, m + i)
                f()

        @block.scalar
        def _(act):
            def empty(dst, src, count):
                act.wait_ge(misc_written, count + 1)
                nc.scalar.activation(dst, src, ACT.Copy).then_inc(misc_emptied, 1)

            def empty_misc(b, kind, slot, place):
                for name, s, a in misc_list(kind):
                    if (s, a) != (slot, place):
                        continue
                    c = misc_count(b, kind, name)
                    if name in ("q1", "next_q0"):
                        empty(qT[0 if name == "next_q0" else 1][:, :], misc[:, :], c)
                    elif name in ("v1", "next_v0"):
                        empty(vals[0 if name == "next_v0" else 1][:, :, :], misc[:, :].rearrange("p (k c) -> p k c", k=NQ), c)
                    elif name in ("prev_recip1", "recip0"):
                        u = 2 * b if name == "recip0" else 2 * b - 1
                        if not (isinstance(u, int) and u == 0):
                            act.wait_ge(ctx_ready, u)
                        empty(inv_cols[:, :], misc[:, :], c)
                    elif name == "prev_hid0":
                        act.wait_ge(hidden_stored, 16 * b)
                        empty(hid[:, 0, :], misc[:, :], c)
                    elif name == "prev_hidT0":
                        empty(hidT[:, 0, :, :], misc[:, :].rearrange("p (k c) -> p k c", k=KT), c)

            def copy_turned(m, i, h):
                act.wait_ge(probs_turned, 4 * m + h + 1)
                if h == 0 and not (isinstance(m, int) and m < 2):
                    act.wait_ge(step_summed, m - 1)
                nc.scalar.activation(probsT[i][:, h, :, :], turn_bank[0][:, :].rearrange("p (k c) -> p k c", k=NQ),
                                     ACT.Copy).then_inc(even_copied, 1)

            def exps(n, i, g, q):
                for h in range(4):
                    if h % 2 == 0:
                        act.wait_ge(neg_max_ready, 2 * n + h // 2 + 1)
                    if not (isinstance(n, int) and n < 2):
                        act.wait_ge(probs_turned, 4 * (n - 2) + h + 1)
                    nc.scalar.activation(probs[i][:, h, :], logit[i][:, h, :], ACT.Exp,
                                         bias=neg_max[:, i, h:h + 1], scale=unit_scale[g][:, q:q + 1],
                                         accum_out=row_sum[:, g, q, h:h + 1]).then_inc(probs_ready, 1)

            empty(wqT[:, :, :], misc[:, :].rearrange("p (k c) -> p k c", k=KD), 0)
            empty(woT[:, :, :], misc[:, :].rearrange("p (k c) -> p k c", k=KD), 1)
            act.wait_ge(misc_written, 3)
            nc.scalar.mul(row_scale[:, :], misc[:, 0:B * NQ], SCALE).then_inc(misc_emptied, 1)
            empty(qT[0][:, :], misc[:, :], 3)
            empty(vals[0][:, :, :], misc[:, :].rearrange("p (k c) -> p k c", k=NQ), 4)

            def body(b, kind):
                for s in range(STEPS):
                    g, q = divmod(s, NQ)
                    n = STEPS * b + s
                    some = kind != FIRST or s >= 1
                    if some:
                        copy_turned(n - 1, (s - 1) % 2, 0)
                    empty_misc(b, kind, s, "A")
                    if some:
                        copy_turned(n - 1, (s - 1) % 2, 2)
                    exps(n, s % 2, g, q)
                    empty_misc(b, kind, s, "B")

            rows(act, body)
            n = STEPS * B
            copy_turned(n - 1, 1, 0)
            copy_turned(n - 1, 1, 2)
            m = misc_last()
            act.wait_ge(ctx_ready, 2 * B - 1)
            empty(inv_cols[:, :], misc[:, :], m)
            act.wait_ge(hidden_stored, 16 * B)
            empty(hid[:, 0, :], misc[:, :], m + 1)
            empty(hidT[:, 0, :, :], misc[:, :].rearrange("p (k c) -> p k c", k=KT), m + 3)

        @block.vector
        def _(dve):
            def empty(dst, src, count):
                dve.wait_ge(misc_written, count + 1)
                nc.vector.tensor_copy(dst, src).then_inc(misc_emptied, 1)

            def row_logits(b):
                return logits_all[:, bass.ds(b * KD, KD), :]

            def empty_misc(b, kind, slot, place):
                for name, s, a in misc_list(kind):
                    if (s, a) != (slot, place):
                        continue
                    c = misc_count(b, kind, name)
                    if name == "prev_hid1":
                        dve.wait_ge(hidden_stored, 16 * b)
                        empty(hid[:, 1, :], misc[:, :], c)
                    elif name == "prev_hidT1":
                        empty(hidT[:, 1, :, :], misc[:, :].rearrange("p (k c) -> p k c", k=KT), c)
                    elif name == "prev_router":
                        empty(row_logits(b - 1), misc[:, 0:KD * E].rearrange("p (k e) -> p k e", k=KD), c)

            def copy_turned(m, i, h):
                dve.wait_ge(probs_turned, 4 * m + h + 1)
                if h == 1 and not (isinstance(m, int) and m < 2):
                    dve.wait_ge(step_summed, m - 1)
                nc.vector.tensor_copy(probsT[i][:, h, :, :], turn_bank[1][:, :].rearrange("p (k c) -> p k c", k=NQ))\
                    .then_inc(odd_copied, 1)

            def maxima(n, i, g, q):
                for h in range(4):
                    dve.wait_ge(logits_written, 4 * n + h + 1)
                    if not (isinstance(n, int) and n < 2):
                        dve.wait_ge(probs_ready, 4 * (n - 2) + h + 1)
                    dve.sem_inc(waits_passed, 1)
                    nc.vector.tensor_tensor_reduce(logit[i][:, h, :], logit_bank[h][:, :], neg_row[g][:, :],
                                                   1.0, LOWEST, ALU.add, ALU.max, row_max[:, i, h:h + 1])\
                        .then_inc(logits_read, 1)
                    if h % 2:
                        dve.wait_ge(logits_read, 4 * n + h + 1)
                        nc.vector.tensor_scalar(neg_max[:, i, h - 1:h + 1], row_max[:, i, h - 1:h + 1],
                                                unit_scale[g][:, q:q + 1], -1.0, ALU.mult, ALU.mult)\
                            .then_inc(neg_max_ready, 1)

            def invert(u, g, n):
                dve.wait_ge(probs_ready, 4 * n + 4)
                nc.vector.reciprocal(inv_sum[:, :, :], row_sum[:, g, :, :].rearrange("p q h -> p (q h)")
                                     .unsqueeze(2).broadcast_to([P, NQ * 4, DK]))\
                    .then_inc(inv_ready, 1)

            def normalise(u, g, n, copied):
                dve.wait_ge(step_summed, n + 1)
                dve.wait_ge(misc_emptied, copied)
                nc.vector.tensor_tensor(ctxn[:, g, :], ctx_bank[:, :], inv_cols[:, :], ALU.mult)\
                    .then_inc(ctx_ready, 1)

            def body(b, kind):
                for s in range(STEPS):
                    g, q = divmod(s, NQ)
                    n = STEPS * b + s
                    some = kind != FIRST or s >= 1
                    if some:
                        copy_turned(n - 1, (s - 1) % 2, 1)
                    if s == 1 and kind != FIRST:
                        invert(2 * b - 1, 1, STEPS * b - 1)
                    if s == NQ + 1:
                        invert(2 * b, 0, STEPS * b + NQ - 1)
                    maxima(n, s % 2, g, q)
                    if s == 2 and kind != FIRST:
                        normalise(2 * b - 1, 1, STEPS * b - 1, misc_count(b, kind, "prev_recip1") + 1)
                    if s == NQ + 2:
                        normalise(2 * b, 0, STEPS * b + NQ - 1, misc_count(b, kind, "recip0") + 1)
                    empty_misc(b, kind, s, "A")
                    if some:
                        copy_turned(n - 1, (s - 1) % 2, 3)
                    empty_misc(b, kind, s, "B")

            rows(dve, body)
            n = STEPS * B
            copy_turned(n - 1, 1, 1)
            copy_turned(n - 1, 1, 3)
            m = misc_last()
            invert(2 * B - 1, 1, n - 1)
            normalise(2 * B - 1, 1, n - 1, m + 1)
            dve.wait_ge(hidden_stored, 16 * B)
            empty(hid[:, 1, :], misc[:, :], m + 2)
            empty(hidT[:, 1, :, :], misc[:, :].rearrange("p (k c) -> p k c", k=KT), m + 4)
            empty(row_logits(B - 1), misc[:, 0:KD * E].rearrange("p (k e) -> p k e", k=KD), m + 5)


        attention.close()

        NT = -(-(2 * TOKENS + E * (P - 1)) // (2 * P)) * 2
        KI = I // P

        def sb(name, shape, dt=F32):
            return ctx.enter_context(nc.sbuf_tensor(name, shape, dt))

        gate_up_sb = sb("gate_up_sb", [P, E * KT, F2])
        down_sb = sb("down_sb", [P, E * KI, T])
        experts_loaded = sem("experts_loaded")
        slot_token = sb("slot_token", [P, NT], I32)
        slot_prob = sb("slot_prob", [P, NT])
        tile_expert = sb("tile_expert", [1, NT], I32)
        token_slot = sb("token_slot", [P, 2, TT], I32)
        expert_rows = nc.dram_tensor("expert_rows_dram", [NT * P, T], F32)

        routing = ExitStack()
        ctx.enter_context(routing)
        with routing:
            def rb(name, shape, dt=F32):
                return routing.enter_context(nc.sbuf_tensor(name, shape, dt))

            expert_no = rb("expert_no", [P, TT, E])
            before_e = rb("before_e", [P, E, E])
            tile_no = rb("tile_no", [P, NT])
            place_no = rb("place_no", [P, P])
            token_no = rb("token_no", [P, TT])
            place_i = rb("place_i", [P, P], I32)
            earlier = rb("earlier", [P, P])
            ones = rb("ones", [P, P])
            best = rb("best", [P, 2, TT])
            chosen = [rb(f"chosen{c}", [P, TT, E]) for c in range(2)]
            rest = rb("rest", [P, TT, E])
            cand = rb("cand", [P, TT, E])
            cand_min = rb("cand_min", [P, TT])
            both = rb("both", [P, TT, E])
            sigm = rb("sigm", [P, 2, TT])
            prob = rb("prob", [P, 2, TT])
            totals = rb("totals", [P, TT, E])
            cum = [rb(f"cum{i}", [P, TT, E]) for i in range(2)]
            slots = rb("slots", [P, TT, E])
            over = rb("over", [P, E, TT])
            tiles_of = rb("tiles_of", [P, E])
            pairs = rb("pairs", [P, E, E])
            first_tile = rb("first_tile", [P, E])
            end_tile = rb("end_tile", [P, E])
            passed = rb("passed", [P, NT, E - 1])
            expert_f = rb("expert_f", [P, NT])
            slot_f = rb("slot_f", [P, 2, TT])
            slot_i = rb("slot_i", [P, 2, TT], I32)
            s_tile_i = rb("s_tile_i", [P, 2, TT], I32)
            s_place_i = rb("s_place_i", [P, 2, TT], I32)
            s_tile = rb("s_tile", [P, 2, TT])
            s_place = rb("s_place", [P, 2, TT])
            at_place = [rb(f"at_place{i}", [P, P]) for i in range(2)]
            at_tile = [rb(f"at_tile{i}", [P, 2, NT]) for i in range(2)]

            def rsem(name):
                return routing.enter_context(nc.semaphore(name))

            constants_ready = rsem("constants_ready")
            chain = rsem("chain")
            best_ready = rsem("best_ready")
            sigm_ready = rsem("sigm_ready")
            both_ready = rsem("both_ready")
            counted = rsem("counted")
            pair_ready = rsem("pair_ready")
            pair_added = rsem("pair_added")
            block2 = routing.enter_context(nc.Block())

            @block2.sync
            def _(sp):
                for e in range(E):
                    sp.dma_start(gate_up_sb[:, e * KT:(e + 1) * KT, :],
                                 gate_up_w[e].rearrange("(k p) f -> p k f", p=P)).then_inc(experts_loaded, 16)
                    sp.dma_start(down_sb[:, e * KI:(e + 1) * KI, :],
                                 down_w[e].rearrange("(k p) d -> p k d", p=P)).then_inc(experts_loaded, 16)

            @block2.gpsimd
            def _(pool):
                kw = dict(allow_small_or_imprecise_dtypes=True)
                nc.gpsimd.iota(expert_no[:, :, :], [[0, TT], [1, E]], base=0, channel_multiplier=0, **kw)
                nc.gpsimd.iota(tile_no[:, :], [[1, NT]], base=0, channel_multiplier=0, **kw)
                nc.gpsimd.iota(place_no[:, :], [[1, P]], base=0, channel_multiplier=0, **kw)
                nc.gpsimd.iota(token_no[:, :], [[P, TT]], base=0, channel_multiplier=1, **kw)
                nc.gpsimd.memset(ones[:, :], 1.0).then_inc(constants_ready, 1)
                nc.gpsimd.memset(before_e[:, :, :], 1.0).then_inc(constants_ready, 1)
                pool.wait_ge(constants_ready, 2)
                nc.gpsimd.affine_select(out=earlier[:, :], in_=ones[:, :], compare_op=ALU.is_gt, fill=0.0,
                                        base=0, pattern=[[1, P]], channel_multiplier=-1)
                nc.gpsimd.affine_select(out=before_e[:, :, :], in_=before_e[:, :, :], compare_op=ALU.is_gt, fill=0.0,
                                        base=0, pattern=[[1, E], [-1, E]], channel_multiplier=0)\
                    .then_inc(constants_ready, 1)

            @block2.scalar
            def _(act):
                act.wait_ge(best_ready, 1)
                nc.scalar.activation(sigm[:, :, :], best[:, :, :], ACT.Exp, scale=-1.0).then_inc(sigm_ready, 1)

            @block2.tensor
            def _(pe):
                pe.wait_ge(constants_ready, 3)
                pe.wait_ge(both_ready, 1)
                flat = both[:, :, :].rearrange("p t e -> p (t e)")
                nc.tensor.matmul(bank[0][:, 0:TT * E], earlier[:, :], flat, start=True, stop=True)
                nc.tensor.matmul(bank[1][:, 0:TT * E], ones[:, :], flat, start=True, stop=True).then_inc(counted, 1)
                for n in range(2 * TT):
                    pe.wait_ge(pair_ready, n + 1)
                    nc.tensor.matmul(bank[2][:, 0:2 * NT], at_place[n % 2][:, :],
                                     at_tile[n % 2][:, :, :].rearrange("p a b -> p (a b)"),
                                     start=(n == 0), stop=(n == 2 * TT - 1)).then_inc(pair_added, 1)

            @block2.vector
            def _(dve):
                done = [0]

                def link(ins):
                    done[0] += 1
                    ins.then_inc(chain, 1)
                    dve.wait_ge(chain, done[0])

                v = nc.vector
                wide = [P, TT, E]
                dve.wait_ge(constants_ready, 3)
                src = logits_all
                for c in range(2):
                    link(v.tensor_reduce(best[:, c, :], src[:, :, :], AX.X, ALU.max))
                    link(v.tensor_tensor(cand[:, :, :], src[:, :, :], best[:, c, :].unsqueeze(2).broadcast_to(wide),
                                         ALU.is_equal))
                    link(v.scalar_tensor_tensor(out=cand[:, :, :], in0=cand[:, :, :], scalar=-float(E),
                                                in1=expert_no[:, :, :], op0=ALU.mult, op1=ALU.add))
                    link(v.tensor_reduce(cand_min[:, :], cand[:, :, :], AX.X, ALU.min))
                    link(v.tensor_tensor(chosen[c][:, :, :], cand[:, :, :],
                                         cand_min[:, :].unsqueeze(2).broadcast_to(wide), ALU.is_equal))
                    if c == 0:
                        link(v.scalar_tensor_tensor(out=rest[:, :, :], in0=chosen[0][:, :, :], scalar=LOWEST,
                                                    in1=logits_all[:, :, :], op0=ALU.mult, op1=ALU.add))
                        src = rest
                v.tensor_tensor(both[:, :, :], chosen[0][:, :, :], chosen[1][:, :, :], ALU.add).then_inc(both_ready, 1)
                v.tensor_copy(cand_min[:, :], best[:, 1, :]).then_inc(best_ready, 1)
                dve.wait_ge(sigm_ready, 1)
                link(v.tensor_scalar(sigm[:, :, :], sigm[:, :, :], 1.0, None, ALU.add))
                link(v.reciprocal(prob[:, :, :], sigm[:, :, :]))
                dve.wait_ge(counted, 1)
                link(v.tensor_copy(totals[:, :, :], bank[1][:, 0:TT * E].rearrange("p (t e) -> p t e", e=E)))
                src, step, i = totals, 1, 0
                while step < TT:
                    v.tensor_copy(cum[i][:, 0:step, :], src[:, 0:step, :])
                    link(v.tensor_tensor(cum[i][:, step:TT, :], src[:, step:TT, :], src[:, 0:TT - step, :], ALU.add))
                    src, step, i = cum[i], 2 * step, 1 - i
                inclusive, spare = src, cum[i]
                link(v.tensor_tensor(spare[:, :, :], inclusive[:, :, :], totals[:, :, :], ALU.subtract))
                link(v.tensor_tensor(slots[:, :, :], spare[:, :, :],
                                     bank[0][:, 0:TT * E].rearrange("p (t e) -> p t e", e=E), ALU.add))
                link(v.tensor_scalar(rest[:, 0, :], inclusive[:, TT - 1, :], 1.0 / P, None, ALU.mult))
                link(v.tensor_tensor(over[:, :, :], rest[:, 0, :].unsqueeze(2).broadcast_to([P, E, TT]),
                                     tile_no[:, 0:TT].unsqueeze(1).broadcast_to([P, E, TT]), ALU.is_gt))
                link(v.tensor_reduce(tiles_of[:, :], over[:, :, :], AX.X, ALU.add))
                link(v.tensor_tensor(pairs[:, :, :], before_e[:, :, :],
                                     tiles_of[:, :].unsqueeze(1).broadcast_to([P, E, E]), ALU.mult))
                link(v.tensor_reduce(first_tile[:, :], pairs[:, :, :], AX.X, ALU.add))
                link(v.tensor_tensor(end_tile[:, :], first_tile[:, :], tiles_of[:, :], ALU.add))
                link(v.tensor_tensor(passed[:, :, :], end_tile[:, 0:E - 1].unsqueeze(1).broadcast_to([P, NT, E - 1]),
                                     tile_no[:, :].unsqueeze(2).broadcast_to([P, NT, E - 1]), ALU.is_le))
                link(v.tensor_reduce(expert_f[:, :], passed[:, :, :], AX.X, ALU.add))
                v.tensor_copy(tile_expert[:, :], expert_f[0:1, :])
                link(v.scalar_tensor_tensor(out=slots[:, :, :],
                                            in0=first_tile[:, :].unsqueeze(1).broadcast_to(wide), scalar=float(P),
                                            in1=slots[:, :, :], op0=ALU.mult, op1=ALU.add))
                for c in range(2):
                    link(v.tensor_tensor(cand[:, :, :], chosen[c][:, :, :], slots[:, :, :], ALU.mult))
                    link(v.tensor_reduce(slot_f[:, c, :], cand[:, :, :], AX.X, ALU.add))
                v.tensor_copy(token_slot[:, :, :], slot_f[:, :, :])
                link(v.tensor_copy(slot_i[:, :, :], slot_f[:, :, :]))
                v.tensor_scalar(s_tile_i[:, :, :], slot_i[:, :, :], P.bit_length() - 1, None, ALU.logical_shift_right)
                link(v.tensor_scalar(s_place_i[:, :, :], slot_i[:, :, :], P - 1, None, ALU.bitwise_and))
                v.tensor_copy(s_tile[:, :, :], s_tile_i[:, :, :])
                link(v.tensor_copy(s_place[:, :, :], s_place_i[:, :, :]))
                for n in range(2 * TT):
                    c, t = divmod(n, TT)
                    if n >= 2:
                        dve.wait_ge(pair_added, n - 1)
                    v.tensor_scalar(at_place[n % 2][:, :], place_no[:, :], s_place[:, c, t:t + 1], None, ALU.is_equal)
                    v.tensor_scalar(at_tile[n % 2][:, 0, :], tile_no[:, :], s_tile[:, c, t:t + 1],
                                    token_no[:, t:t + 1], ALU.is_equal, ALU.mult)
                    v.tensor_scalar(at_tile[n % 2][:, 1, :], tile_no[:, :], s_tile[:, c, t:t + 1],
                                    prob[:, c, t:t + 1], ALU.is_equal, ALU.mult).then_inc(pair_ready, 1)
                dve.wait_ge(pair_added, 2 * TT)
                v.tensor_copy(slot_token[:, :], bank[2][:, 0:NT])
                v.tensor_copy(slot_prob[:, :], bank[2][:, NT:2 * NT])

        experts = ExitStack()
        ctx.enter_context(experts)
        with experts:
            def eb(name, shape, dt=F32):
                return [experts.enter_context(nc.sbuf_tensor(f"{name}{i}", shape, dt)) for i in range(2)]

            def esem(name):
                return experts.enter_context(nc.semaphore(name))

            row_no = eb("row_no", [P, 1], I32)
            row_prob = eb("row_prob", [P, 1])
            rows_in = eb("rows_in", [P, T])
            rows_scaled = eb("rows_scaled", [P, T])
            rows_T = eb("rows_T", [P, KT, P])
            gated = eb("gated", [P, I])
            act_h = eb("act_h", [P, I])
            act_hT = eb("act_hT", [P, KI, P])
            rows_out = eb("rows_out", [P, T])
            inT_bank, gu_bank, hT_bank, out_bank = bank[0:2], bank[2:4], bank[4:6], bank[6:8]

            gathered = [esem(f"gathered{i}") for i in range(2)]
            row_no_ready = esem("row_no_ready")
            scaled = esem("scaled")
            in_turned = esem("in_turned")
            in_copied = esem("in_copied")
            gu_done = esem("gu_done")
            silu_done = esem("silu_done")
            h_done = esem("h_done")
            h_turned = esem("h_turned")
            h_copied = esem("h_copied")
            down_done = esem("down_done")
            out_copied = esem("out_copied")
            stored = [esem(f"stored{i}") for i in range(2)]
            block3 = experts.enter_context(nc.Block())

            def tiles(eng, body):
                for i in range(2):
                    body(i, i, True)
                with eng.Fori(1, NT // 2) as n:
                    for i in range(2):
                        body(2 * n + i, i, False)

            def ready(n, i, first):
                return 16 if first else 8 * (n - i) + 16

            @block3.gpsimd
            def _(pool):
                def body(n, i, first):
                    if not first:
                        pool.wait_ge(scaled, n - 1)
                    nc.gpsimd.tensor_copy(row_prob[i][:, :], slot_prob[:, bass.ds(n, 1)])
                    nc.gpsimd.tensor_copy(row_no[i][:, :], slot_token[:, bass.ds(n, 1)]).then_inc(row_no_ready, 1)
                    pool.wait_ge(row_no_ready, n + 1)
                    pool.sem_inc(pool_waits_passed, 1)
                    nc.gpsimd.indirect_dma_start(rows_in[i][:, :], None, hidden[:, :],
                                                 bass.IndirectOffsetOnAxis(ap=row_no[i][:, 0:1], axis=0))\
                        .then_inc(gathered[i], 16)
                tiles(pool, body)

            @block3.vector
            def _(dve):
                def scale_rows(n, i, first):
                    dve.wait_ge(gathered[i], ready(n, i, first))
                    if not first:
                        dve.wait_ge(in_turned, n - 1)
                    nc.vector.tensor_scalar(rows_scaled[i][:, :], rows_in[i][:, :], row_prob[i][:, 0:1], None, ALU.mult)\
                        .then_inc(scaled, 1)

                def combine(n, i, first):
                    dve.wait_ge(silu_done, n + 1)
                    if not first:
                        dve.wait_ge(h_turned, n - 1)
                    nc.vector.tensor_tensor(act_h[i][:, :], gated[i][:, :], gu_bank[i][:, I:F2], ALU.mult)\
                        .then_inc(h_done, 1)

                def copy_h(n, i, first):
                    dve.wait_ge(h_turned, n + 1)
                    if not first:
                        dve.wait_ge(down_done, n - 1)
                    nc.vector.tensor_copy(act_hT[i][:, :, :],
                                          hT_bank[i][:, 0:I].rearrange("p (k c) -> p k c", k=KI)).then_inc(h_copied, 1)

                def body(n, i, first):
                    scale_rows(n, i, first)
                    combine(n, i, first)
                    copy_h(n, i, first)
                tiles(dve, body)

            @block3.scalar
            def _(act):
                def copy_in(n, i, first):
                    act.wait_ge(in_turned, n + 1)
                    if not first:
                        act.wait_ge(gu_done, n - 1)
                    nc.scalar.activation(rows_T[i][:, :, :], inT_bank[i][:, :].rearrange("p (k c) -> p k c", k=KT),
                                         ACT.Copy).then_inc(in_copied, 1)

                def silu(n, i, first):
                    act.wait_ge(gu_done, n + 1)
                    if not first:
                        act.wait_ge(h_done, n - 1)
                    nc.scalar.activation(gated[i][:, :], gu_bank[i][:, 0:I], ACT.Silu).then_inc(silu_done, 1)

                def copy_out(n, i, first):
                    act.wait_ge(down_done, n + 1)
                    if not first:
                        act.wait_ge(stored[i], 8 * (n - i))
                    nc.scalar.activation(rows_out[i][:, :], out_bank[i][:, :], ACT.Copy).then_inc(out_copied, 1)

                copy_in(0, 0, True)
                silu(0, 0, True)
                copy_in(1, 1, True)
                silu(1, 1, True)
                copy_out(0, 0, True)
                with act.Fori(1, NT // 2) as n:
                    copy_in(2 * n, 0, False)
                    silu(2 * n, 0, False)
                    act.wait_ge(down_done, 2 * n)
                    act.wait_ge(stored[1], 16 * n)
                    nc.scalar.activation(rows_out[1][:, :], out_bank[1][:, :], ACT.Copy).then_inc(out_copied, 1)
                    copy_in(2 * n + 1, 1, False)
                    silu(2 * n + 1, 1, False)
                    copy_out(2 * n, 0, False)
                act.wait_ge(down_done, NT)
                act.wait_ge(stored[1], 8 * NT)
                nc.scalar.activation(rows_out[1][:, :], out_bank[1][:, :], ACT.Copy).then_inc(out_copied, 1)

            @block3.sync
            def _(sp):
                sp.sem_inc(stored[1], 16)
                def body(n, i, first):
                    sp.wait_ge(out_copied, n + 1)
                    sp.dma_start(expert_rows[bass.ds(n * P, P), :], rows_out[i][:, :]).then_inc(stored[i], 16)
                tiles(sp, body)
                for i in range(2):
                    sp.wait_ge(stored[i], 8 * NT + 16 * i)

            @block3.tensor
            def _(pe):
                pe.wait_ge(experts_loaded, 2 * E * 16)

                def turn_in(n, i, first):
                    pe.wait_ge(scaled, n + 1)
                    if not first:
                        pe.wait_ge(in_copied, n - 1)
                    for k in range(KT):
                        last = nc.tensor.transpose(inT_bank[i][:, k * P:(k + 1) * P],
                                                   rows_scaled[i][:, k * P:(k + 1) * P], ident[:, :])
                    last.then_inc(in_turned, 1)

                def gate_up(n, i, first, e):
                    pe.wait_ge(in_copied, n + 1)
                    if not first:
                        pe.wait_ge(h_done, n - 1)
                    for k in range(KT):
                        w = gate_up_sb[:, bass.ds(e * KT + k, 1), :].rearrange("p o f -> p (o f)")
                        last = nc.tensor.matmul(gu_bank[i][:, :], rows_T[i][:, k, :], w,
                                                start=(k == 0), stop=(k == KT - 1))
                    last.then_inc(gu_done, 1)

                def turn_h(n, i, first):
                    pe.wait_ge(h_done, n + 1)
                    if not first:
                        pe.wait_ge(h_copied, n - 1)
                    for k in range(KI):
                        last = nc.tensor.transpose(hT_bank[i][:, k * P:(k + 1) * P],
                                                   act_h[i][:, k * P:(k + 1) * P], ident[:, :])
                    last.then_inc(h_turned, 1)

                def down(n, i, first, e):
                    pe.wait_ge(h_copied, n + 1)
                    if not first:
                        pe.wait_ge(out_copied, n - 1)
                    for k in range(KI):
                        w = down_sb[:, bass.ds(e * KI + k, 1), :].rearrange("p o f -> p (o f)")
                        last = nc.tensor.matmul(out_bank[i][:, :], act_hT[i][:, k, :], w,
                                                start=(k == 0), stop=(k == KI - 1))
                    last.then_inc(down_done, 1)

                def body(n, i, first):
                    e = pe.value_load(tile_expert[0:1, bass.ds(n, 1)], min_val=0, max_val=E - 1)
                    turn_in(n, i, first)
                    gate_up(n, i, first, e)
                    turn_h(n, i, first)
                    down(n, i, first, e)
                tiles(pe, body)

        shared = ExitStack()
        ctx.enter_context(shared)
        with shared:
            def fb(name, shape, dt=F32):
                return [shared.enter_context(nc.sbuf_tensor(f"{name}{i}", shape, dt)) for i in range(2)]

            def fsem(name):
                return shared.enter_context(nc.semaphore(name))

            tok = fb("tok", [P, KD, T])
            tokT = shared.enter_context(nc.sbuf_tensor("tokT", [P, KT, D], F32))
            sgate = shared.enter_context(nc.sbuf_tensor("sgate", [P, KI, D], F32))
            sh = shared.enter_context(nc.sbuf_tensor("sh", [P, KI, D], F32))
            slot_no = [fb(f"slot_no{c}_", [P, 1], I32) for c in range(2)]
            expert_row = [fb(f"expert_row{c}_", [P, T]) for c in range(2)]
            total = fb("total", [P, T])
            tok_loaded = [fsem(f"tok_loaded{i}") for i in range(2)]
            tok_turned = fsem("tok_turned")
            tokT_copied = fsem("tokT_copied")
            up_done = fsem("up_done")
            sgate_done = fsem("sgate_done")
            sh_done = fsem("sh_done")
            shared_done = fsem("shared_done")
            slot_no_ready = fsem("slot_no_ready")
            row_gathered = [fsem(f"row_gathered{i}") for i in range(2)]
            part_added = fsem("part_added")
            row_sum_ready = fsem("row_sum_ready")
            total_ready = fsem("total_ready")
            out_stored = [fsem(f"out_stored{i}") for i in range(2)]
            block4 = shared.enter_context(nc.Block())

            def row_pairs(eng, body):
                for i in range(2):
                    body(i, i, True)
                with eng.Fori(1, B // 2) as n:
                    for i in range(2):
                        body(2 * n + i, i, False)

            out_rows = out.rearrange("b d t -> (b d) t")

            @block4.sync
            def _(sp):
                def load(b, i):
                    sp.dma_start(tok[i][:, :, :], hidden[bass.ds(b * D, D), :].rearrange("(k p) t -> p k t", p=P))\
                        .then_inc(tok_loaded[i], 16)

                def body(b, i, first):
                    if not first:
                        sp.wait_ge(tok_turned, 2 * (b - 1))
                    load(b, i)
                row_pairs(sp, body)

            @block4.scalar
            def _(act):
                def body(b, i, first):
                    for h in range(2):
                        act.wait_ge(tok_turned, 2 * b + h + 1)
                        if h == 0 and not (isinstance(b, int) and b == 0):
                            act.wait_ge(up_done, b)
                        nc.scalar.activation(tokT[:, 2 * h:2 * h + 2, :],
                                             bank[h][:, :].rearrange("p (k c) -> p k c", k=2), ACT.Copy)\
                            .then_inc(tokT_copied, 1)
                    act.wait_ge(up_done, b + 1)
                    if not (isinstance(b, int) and b == 0):
                        act.wait_ge(sh_done, b)
                    nc.scalar.activation(sgate[:, :, :], bank[2][:, :].rearrange("p (k c) -> p k c", k=KI), ACT.Silu)\
                        .then_inc(sgate_done, 1)
                    for h in range(KD):
                        n = 2 * b + h
                        act.wait_ge(total_ready, n + 1)
                        act.dma_start(out_rows[bass.ds(n * P, P), :], total[h][:, :]).then_inc(out_stored[h], 16)
                row_pairs(act, body)
                for h in range(KD):
                    act.wait_ge(out_stored[h], 16 * B)

            @block4.tensor
            def _(pe):
                pe.wait_ge(shared_loaded, 48)

                def body(b, i, first):
                    later = not (isinstance(b, int) and b == 0)
                    pe.wait_ge(tok_loaded[i], 16 if first else 8 * (b - i) + 16)
                    for h in range(2):
                        if later:
                            pe.wait_ge(tokT_copied, 2 * b - 1 + h)
                        for k in range(2):
                            for m in range(KD):
                                c = k * D + m * P
                                last = nc.tensor.transpose(bank[h][:, c:c + P],
                                                           tok[i][:, m, (2 * h + k) * P:(2 * h + k + 1) * P], ident[:, :])
                        last.then_inc(tok_turned, 1)
                    pe.wait_ge(tokT_copied, 2 * b + 2)
                    if later:
                        pe.wait_ge(sh_done, b)
                    for w, dst in zip(shared_in, bank[2:4]):
                        for m in range(KI):
                            for k in range(KT):
                                last = nc.tensor.matmul(dst[:, m * D:(m + 1) * D], w[:, k, m * P:(m + 1) * P],
                                                        tokT[:, k, :], start=(k == 0), stop=(k == KT - 1))
                    last.then_inc(up_done, 1)
                    pe.wait_ge(sh_done, b + 1)
                    for h in range(KD):
                        if later:
                            pe.wait_ge(part_added, 2 * b - 1 + h)
                        for k in range(KI):
                            last = nc.tensor.matmul(bank[4 + h][:, :], sh[:, k, h * P:(h + 1) * P], shared_out[:, k, :],
                                                    start=(k == 0), stop=(k == KI - 1))
                        last.then_inc(shared_done, 1)
                row_pairs(pe, body)

            @block4.gpsimd
            def _(pool):
                def body(b, i, first):
                    for h in range(KD):
                        n = 2 * b + h
                        if not (isinstance(b, int) and b == 0):
                            pool.wait_ge(total_ready, n - 1)
                        for c in range(2):
                            nc.gpsimd.tensor_copy(slot_no[c][h][:, :], token_slot[:, c, bass.ds(n, 1)])\
                                .then_inc(slot_no_ready, 1)
                        pool.wait_ge(slot_no_ready, 2 * n + 2)
                        pool.sem_inc(pool_waits_passed, 1)
                        for c in range(2):
                            nc.gpsimd.indirect_dma_start(expert_row[c][h][:, :], None, expert_rows[:, :],
                                                         bass.IndirectOffsetOnAxis(ap=slot_no[c][h][:, 0:1], axis=0))\
                                .then_inc(row_gathered[h], 16)
                row_pairs(pool, body)

            @block4.vector
            def _(dve):
                def body(b, i, first):
                    dve.wait_ge(sgate_done, b + 1)
                    if not (isinstance(b, int) and b == 0):
                        dve.wait_ge(shared_done, 2 * b)
                    nc.vector.tensor_tensor(sh[:, :, :], sgate[:, :, :],
                                            bank[3][:, :].rearrange("p (k c) -> p k c", k=KI), ALU.mult)\
                        .then_inc(sh_done, 1)
                    for h in range(KD):
                        n = 2 * b + h
                        dve.wait_ge(shared_done, n + 1)
                        if not (isinstance(b, int) and b == 0):
                            dve.wait_ge(out_stored[h], 16 * b)
                        xs = x_all[:, bass.ds(n, 1), :].rearrange("p o t -> p (o t)")
                        nc.vector.tensor_tensor(total[h][:, :], bank[4 + h][:, :], xs, ALU.add).then_inc(part_added, 1)
                        dve.wait_ge(row_gathered[h], 32 * (b + 1))
                        nc.vector.tensor_tensor(expert_row[1][h][:, :], expert_row[0][h][:, :], expert_row[1][h][:, :],
                                                ALU.add).then_inc(row_sum_ready, 1)
                        dve.wait_ge(row_sum_ready, n + 1)
                        dve.wait_ge(part_added, n + 1)
                        nc.vector.tensor_tensor(total[h][:, :], total[h][:, :], expert_row[1][h][:, :], ALU.add)\
                            .then_inc(total_ready, 1)
                row_pairs(dve, body)



_INS = ["x", "cond_2048", "L0_cond_Wq", "L0_cond_Wo", "L0_ffn_router_w", "L0_ffn_gate_up_w", "L0_ffn_down_w",
        "L0_ffn_shared_gate_w", "L0_ffn_shared_up_w", "L0_ffn_shared_down_w"]


def kernel(**inputs):
    import numpy as np
    import concourse.bacc as bacc
    from concourse.bass_utils import run_bass_kernel_spmd

    nc = bacc.Bacc("TRN2", target_bir_lowering=False, num_devices=1)
    arrays, args = {}, []
    for name in _INS:
        a = np.ascontiguousarray(inputs[name])
        arrays[f"in_{name}"] = a
        args.append(nc.dram_tensor(f"in_{name}", a.shape, mybir.dt.from_np(a.dtype), kind="ExternalInput").ap())
    shape = inputs["x"].shape
    args.append(nc.dram_tensor("out_0", shape, F32, kind="ExternalOutput").ap())
    build(nc, *args)
    r = run_bass_kernel_spmd(nc, [arrays], core_ids=[0])
    return r.results[0]["out_0"]
```

```python
from contextlib import ExitStack

import numpy as np

import concourse.bass as bass
from concourse import mybir

ALU = mybir.AluOpType
ACT = mybir.ActivationFunctionType
AX = mybir.AxisListType
F32 = mybir.dt.float32
F32R = mybir.dt.float32r
I32 = mybir.dt.int32

P = 128
BANK = 512
DK = 32
NEG = -1e30
LOWEST = -3.0e38

FIRST, MIDDLE, LAST = range(3)
MISC = [("k1_0", 0, 0), ("q1_0", 1, 1), ("k1_1", 2, 0), ("prev_ctx1_1", 3, 1), ("q1_1", 4, 0), ("max0_1", 4, 1), ("next_q0", 5, 0),
        ("prev_normed1", 6, 1), ("prev_hid0", 6, 0), ("prev_hid1", 7, 1), ("k1_2", 9, 1),
        ("q1_2", 10, 0), ("prev_hidT0", 10, 1), ("ctx0_0", 11, 0), ("k1_3", 12, 1), ("max1_0", 12, 0),
        ("q1_3", 13, 1), ("prev_hidT1", 14, 0),
        ("k0_0", 16, 0), ("q0_0", 17, 1), ("k0_1", 18, 0), ("ctx0_1", 19, 1), ("q0_1", 20, 0), ("max1_1", 20, 1),
        ("normed0", 22, 1), ("prev_router", 22, 0), ("next_q1", 23, 0), ("k0_2", 25, 1), ("q0_2", 26, 0),
        ("ctx1_0", 27, 0), ("k0_3", 28, 1), ("next_max0_0", 28, 0), ("q0_3", 29, 1)]
MISC_SETUP = [("wqT", 0), ("woT", 1), ("maskT", 0), ("q0", 0)]     + [(f"s0{c}_{h}", i) for h in range(4) for i, c in enumerate("kq")] + [("q1", 0), ("max0", 1)]
MISC_TAIL = [("tail_ctx1", 0), ("tail_normed", 1), ("tail_hid0", 0), ("tail_hid1", 1), ("tail_hidT0", 1),
             ("tail_hidT1", 0), ("tail_router", 1)]
BANK_OF = dict([(m[0], m[-1]) for m in MISC + MISC_SETUP + MISC_TAIL])


def misc_list(kind):
    return [m for m in MISC
            if not (kind == FIRST and m[0].startswith("prev"))
            and not (kind == LAST and (m[0].startswith("next") or m[0][:2] in ("k0", "q0")))]


def in_bank(uses, name):
    return [m[0] for m in uses if m[-1] == BANK_OF[name]]


def misc_count(b, kind, name):
    before = len(in_bank(MISC_SETUP, name))
    if kind != FIRST:
        before = before + len(in_bank(misc_list(FIRST), name)) + len(in_bank(misc_list(MIDDLE), name)) * (b - 1)
    return before + in_bank(misc_list(kind), name).index(name)


def setup_count(name):
    return in_bank(MISC_SETUP, name).index(name)


def tail_count(rows, name):
    return len(in_bank(MISC_SETUP, name)) + len(in_bank(misc_list(FIRST), name)) + len(in_bank(misc_list(LAST), name)) \
        + len(in_bank(misc_list(MIDDLE), name)) * (rows - 2) + in_bank(MISC_TAIL, name).index(name)


def fp32r(value):
    return float((np.float32(value).view(np.uint32) & np.uint32(0xFFFFF000)).view(np.float32))


def build(nc, x, cond, wq, wo, router_w, gate_up_w, down_w, sh_gate_w, sh_up_w, sh_down_w, out, stop_after=9):
    B, D, T = x.shape
    E, _, F2 = gate_up_w.shape
    I = F2 // 2
    KD = D // P
    KT = T // P
    NQ = T // P
    G = D // P
    TOKENS = B * D
    TT = TOKENS // P
    SCALE = float(DK) ** -0.5
    assert T == BANK and KD == G == 2

    ctx = ExitStack()
    with ctx:
        def sb(name, shape, dt=F32):
            return ctx.enter_context(nc.sbuf_tensor(name, shape, dt))

        def sem(name):
            return ctx.enter_context(nc.semaphore(name))

        first_banks = ctx.enter_context(nc.psum_tensor("first_banks", [P, 2, BANK], F32))
        bank = [first_banks[:, i, :] for i in range(2)]
        bank += [ctx.enter_context(nc.psum_tensor(f"bank{i}", [P, BANK], F32)) for i in range(2, 8)]
        hidden = nc.dram_tensor("hidden_dram", [TOKENS, T], F32)

        ident = sb("ident", [P, P])
        logits_all = sb("logits_all", [P, TT, E])
        shared_in = [sb(f"shared_in{i}", [P, KT, I]) for i in range(2)]
        shared_out = sb("shared_out", [P, I // P, T])
        shared_loaded = sem("shared_loaded")

        attention = ExitStack()
        ctx.enter_context(attention)

        def sb(name, shape, dt=F32):
            return attention.enter_context(nc.sbuf_tensor(name, shape, dt))

        HPU = 4
        NJ = HPU * NQ
        BIAS_ROWS = 5
        MASK_ONE = 2.0 ** 50
        MASK_NEG = fp32r(NEG / SCALE / BIAS_ROWS / MASK_ONE)
        LOGIT_STEPS = (0, 1, 2, 3)
        R_MASK, R_MAX = 3 * DK, 3 * DK + BIAS_ROWS
        K_MAX, K_ALL = R_MAX, R_MAX + 2

        logit_bank, key_bank, ctx_bank, misc = bank[0:2], bank[2:4], bank[4:6], bank[6:8]
        w_nat = sb("w_nat", [P, 2, KD, D])
        wqT = sb("wqT", [P, KD, D])
        woT = sb("woT", [P, KD, D])
        router_sb = sb("router_sb", [P, KT, E])
        x_row = sb("x_row", [P, KD, T])
        mask_nat = sb("mask_nat", [B * NQ, P])
        mask_cols = sb("mask_cols", [P, B * NQ])
        mask_now = sb("mask_now", [P, NQ])
        q_nat = sb("q_nat", [P, NQ, P])
        qm = sb("qm", [P, NQ, P])
        q_cols = [sb(f"q_cols{g}", [P, NQ, HPU, P]) for g in range(G)]
        k_cols = [sb(f"k_cols{g}", [P, NQ, HPU, P]) for g in range(G)]
        q_stack = [sb(f"q_stack{g}", [P, HPU, T], F32R) for g in range(G)]
        k_stack = [sb(f"k_stack{g}", [P, HPU, T], F32R) for g in range(G)]
        vals = [sb(f"vals{g}", [P, NQ, HPU, 2 * DK]) for g in range(G)]
        row_max = [sb(f"row_max{g}", [P, NJ]) for g in range(G)]
        max_hi = sb("max_hi", [2 * NQ, P], F32R)
        max_lo = sb("max_lo", [2 * NQ, P], F32R)
        probsT = [sb(f"probsT{i}", [P, T]) for i in range(4)]
        ctx_raw = [sb(f"ctx_raw{i}", [P, T]) for i in range(2)]
        inv_sum = [sb(f"inv_sum{i}", [P, NQ, 2]) for i in range(2)]
        ctx_nat = sb("ctx_nat", [P, NQ, HPU, DK])
        ctxn = sb("ctxn", [P, G, T])
        hid = sb("hid", [P, KD, T])
        hidT = sb("hidT", [P, KD, KT, P])

        x_loaded = sem("x_loaded")
        weights_loaded = [sem(f"weights_loaded{i}") for i in range(2)]
        router_loaded = sem("router_loaded")
        mask_loaded = sem("mask_loaded")
        max_loaded = [sem(f"max_loaded{g}") for g in range(G)]
        ident_cleared = sem("ident_cleared")
        ident_ready = sem("ident_ready")
        ones_ready = sem("ones_ready")
        written = [sem(f"misc_written{i}") for i in range(2)]
        emptied = [sem(f"misc_emptied{i}") for i in range(2)]
        vals_ready = sem("vals_ready")
        cols_cleared = sem("cols_cleared")
        mask_copied = sem("mask_copied")
        cols_ready = sem("cols_ready")
        qm_ready = sem("qm_ready")
        hi_ready = sem("hi_ready")
        logits_written = sem("logits_written")
        logits_reduced = sem("logits_reduced")
        max_hi_ready = sem("max_hi_ready")
        keys_written = sem("keys_written")
        probs_ready = sem("probs_ready")
        weighed = sem("weighed")
        ctx_copied = sem("ctx_copied")
        inv_ready = sem("inv_ready")
        hidden_stored = sem("hidden_stored")
        pool_waits_passed = sem("pool_waits_passed")
        sp_waits_passed = sem("sp_waits_passed")

        block = attention.enter_context(nc.Block())

        def rows(eng, body):
            body(0, FIRST)
            with eng.Fori(1, B - 1) as b:
                body(b, MIDDLE)
            body(B - 1, LAST)

        def is_int(n, m):
            return isinstance(n, int) and n == m

        def tail(name):
            return tail_count(B, name)

        def four(m):
            return m[:, :].rearrange("p (k c) -> p k c", c=P)

        @block.sync
        def _(sp):
            def load_max(b, g, two, name, count):
                i = BANK_OF[name]
                sp.wait_ge(emptied[i], count + 1)
                for i, part in enumerate((max_hi, max_lo)):
                    dst = q_stack[g][R_MAX + i:R_MAX + i + 1, 2 * two:2 * two + 2, :]
                    sp.dma_start(dst.bitcast(F32).rearrange("o h (q p) -> o (h q) p", p=P), part[:, :].bitcast(F32))\
                        .then_inc(max_loaded[g], 16)

            def store_hidden(b, copied):
                for i in range(2):
                    sp.wait_ge(emptied[i], copied[i])
                    sp.sem_inc(sp_waits_passed, 1)
                sp.dma_start(hidden[bass.ds(b * D, D), :].rearrange("(k p) t -> p k t", p=P), hid[:, :, :])\
                    .then_inc(hidden_stored, 16)

            sp.sem_inc(hidden_stored, 16)
            sp.dma_start(w_nat[:, 0, :, :], wq.rearrange("(m p) d -> p m d", p=P)).then_inc(weights_loaded[0], 16)
            sp.dma_start(x_row[:, :, :], x[0].rearrange("(k p) t -> p k t", p=P)).then_inc(x_loaded, 16)
            sp.dma_start(mask_nat[:, :], cond.rearrange("b (q p) -> (b q) p", p=P)).then_inc(mask_loaded, 16)
            sp.dma_start(w_nat[:, 1, :, :], wo.rearrange("(m p) d -> p m d", p=P)).then_inc(weights_loaded[1], 16)
            sp.dma_start(router_sb[:, :, :], router_w.rearrange("(k p) e -> p k e", p=P)).then_inc(router_loaded, 16)
            load_max(0, 0, 0, "max0", setup_count("max0"))
            for dst, src in zip(shared_in, (sh_gate_w, sh_up_w)):
                sp.dma_start(dst[:, :, :], src.rearrange("(k p) i -> p k i", p=P)).then_inc(shared_loaded, 16)
            sp.dma_start(shared_out[:, :, :], sh_down_w.rearrange("(k p) d -> p k d", p=P)).then_inc(shared_loaded, 16)

            def body(b, kind):
                if kind != LAST:
                    sp.wait_ge(qm_ready, 2 * b + 2)
                    sp.sem_inc(sp_waits_passed, 1)
                    sp.dma_start(x_row[:, :, :], x[bass.ds(b + 1, 1)].rearrange("o (k p) t -> p (o k) t", p=P))\
                        .then_inc(x_loaded, 16)
                load_max(b, 0, 1, "max0_1", misc_count(b, kind, "max0_1"))
                if kind != FIRST:
                    store_hidden(b - 1, [misc_count(b, kind, f"prev_hid{i}") + 1 for i in range(2)])
                load_max(b, 1, 0, "max1_0", misc_count(b, kind, "max1_0"))
                load_max(b, 1, 1, "max1_1", misc_count(b, kind, "max1_1"))
                if kind != LAST:
                    load_max(b + 1, 0, 0, "next_max0_0", misc_count(b, kind, "next_max0_0"))

            rows(sp, body)
            store_hidden(B - 1, [tail(f"tail_hid{i}") + 1 for i in range(2)])
            sp.wait_ge(hidden_stored, 16 * B + 16)

        @block.gpsimd
        def _(pool):
            nc.gpsimd.memset(ident[:, :], 0.0).then_inc(ident_cleared, 1)
            pool.wait_ge(ident_cleared, 1)
            nc.gpsimd.affine_select(out=ident[:, :], in_=ident[:, :], compare_op=ALU.not_equal, fill=1.0,
                                    base=0, pattern=[[-1, P]], channel_multiplier=1).then_inc(ident_ready, 1)

            def split(b, g, name, copied):
                u = 2 * b + g
                if not is_int(u, 0):
                    pool.wait_ge(cols_ready, 4 * u)
                    pool.sem_inc(pool_waits_passed, 1)
                nc.gpsimd.tensor_copy(mask_now[:, :], mask_cols[:, bass.ds(b * NQ, NQ)]).then_inc(mask_copied, 1)
                pool.wait_ge(mask_copied, u + 1)
                pool.wait_ge(emptied[BANK_OF[name]], copied)
                nc.gpsimd.tensor_tensor(qm[:, :, :], q_nat[:, :, :],
                                        mask_now[:, :].unsqueeze(2).broadcast_to([P, NQ, P]), ALU.mult)\
                    .then_inc(qm_ready, 1)
                m = mask_now[:, :].unsqueeze(2).unsqueeze(3).broadcast_to([P, NQ, HPU, BIAS_ROWS])
                nc.gpsimd.tensor_scalar(q_cols[g][:, :, :, R_MASK:R_MAX], m, MASK_ONE, None, ALU.mult)\
                    .then_inc(cols_ready, 1)
                nc.gpsimd.tensor_scalar(k_cols[g][:, :, :, R_MASK:R_MAX], m, -MASK_NEG, MASK_NEG, ALU.mult, ALU.add)\
                    .then_inc(cols_ready, 1)
                pool.wait_ge(hi_ready, 4 * u + 4)
                whole = qm[:, :, :].rearrange("p k (h d) -> p k h d", h=HPU)
                for cols, at in ((q_cols[g], DK), (k_cols[g], 2 * DK)):
                    nc.gpsimd.tensor_tensor(cols[:, :, :, at:at + DK], whole, q_cols[g][:, :, :, 0:DK], ALU.subtract)\
                        .then_inc(cols_ready, 1)

            def values(u, g, steps_before):
                if steps_before is not None:
                    pool.wait_ge(weighed, steps_before)
                    pool.sem_inc(pool_waits_passed, 1)
                nc.gpsimd.tensor_copy(vals[g][:, :, :, 0:DK], q_nat[:, :, :].rearrange("p k (h d) -> p k h d", h=HPU))\
                    .then_inc(vals_ready, 1)

            pool.wait_ge(cols_cleared, 4)
            pool.wait_ge(emptied[BANK_OF["maskT"]], setup_count("maskT") + 1)
            split(0, 0, "q0", setup_count("q0") + 1)
            values(0, 0, None)
            split(0, 1, "q1", setup_count("q1") + 1)

            def body(b, kind):
                values(2 * b + 1, 1, None if kind == FIRST else 2 * NJ * b)
                if kind != LAST:
                    split(b + 1, 0, "next_q0", misc_count(b, kind, "next_q0") + 1)
                    values(2 * b + 2, 0, 2 * NJ * b + NJ)
                    split(b + 1, 1, "next_q1", misc_count(b, kind, "next_q1") + 1)

            rows(pool, body)

        @block.tensor
        def _(pe):
            def turn(dst, src, n=P):
                return nc.tensor.transpose(dst, src, ident[0:n, 0:n])

            def turn_blocks(dst, src, n):
                for k in range(n):
                    last = turn(dst[:, k * P:(k + 1) * P], src(k))
                return last

            def project_q(m, b, g):
                pe.wait_ge(x_loaded, 16 * (b + 1))
                for q in range(NQ):
                    for k in range(KD):
                        last = nc.tensor.matmul(m[:, q * P:(q + 1) * P], x_row[:, k, q * P:(q + 1) * P],
                                                wqT[:, k, g * P:(g + 1) * P], start=(k == 0), stop=(k == KD - 1))
                return last

            def turn_cols(m, u, cols, h):
                pe.wait_ge(hi_ready, 4 * u + 4)
                pe.wait_ge(cols_ready, 4 * u + 4)
                return turn_blocks(m, lambda k: cols[:, k, h, :], NQ)

            def turn_max(m, u, g, two):
                pe.wait_ge(logits_reduced, 8 * u + 4 * two + 4)
                return turn(m[0:2 * NQ, 0:P], row_max[g][:, 2 * NQ * two:2 * NQ * (two + 1)])

            def turn_ctx(m, u, two):
                pe.wait_ge(ctx_copied, 2 * u + two + 1)
                return turn_blocks(m, lambda k: ctx_raw[two][:, k * P:(k + 1) * P], NQ)

            def turn_normed(m, name, count):
                pe.wait_ge(emptied[BANK_OF[name]], count)
                return turn_blocks(m, lambda k: ctx_nat[:, k, :, :].rearrange("p h d -> p (h d)"), NQ)

            def hidden_half(m, e, copied):
                pe.wait_ge(emptied[BANK_OF["prev_normed1"]], copied)
                for g in range(G):
                    last = nc.tensor.matmul(m[:, :], woT[:, g, e * P:(e + 1) * P], ctxn[:, g, :],
                                            start=(g == 0), stop=(g == G - 1))
                return last

            def turn_hidden(m, e, copied):
                pe.wait_ge(emptied[BANK_OF[f"prev_hid{e}"]], copied)
                return turn_blocks(m, lambda k: hid[:, e, k * P:(k + 1) * P], KT)

            def route(m, copied):
                for e in range(KD):
                    pe.wait_ge(emptied[BANK_OF[f"prev_hidT{e}"]], copied[e])
                    for k in range(KT):
                        last = nc.tensor.matmul(m[:, e * E:(e + 1) * E], hidT[:, e, k, :], router_sb[:, k, :],
                                                start=(k == 0), stop=(k == KT - 1))
                return last

            def use(name, count, f, *args):
                i = BANK_OF[name]
                if not is_int(count, 0):
                    pe.wait_ge(emptied[i], count)
                f(misc[i], *args).then_inc(written[i], 1)

            def use_misc(b, kind, slot):
                for name, s, _ in misc_list(kind):
                    if s != slot:
                        continue
                    c = misc_count(b, kind, name)
                    u = 2 * b
                    done = lambda n: misc_count(b, kind, n) + 1
                    job = {
                        "prev_ctx1_1": (turn_ctx, u - 1, 1), "ctx0_0": (turn_ctx, u, 0),
                        "ctx0_1": (turn_ctx, u, 1), "ctx1_0": (turn_ctx, u + 1, 0),
                        "max0_1": (turn_max, u, 0, 1), "max1_0": (turn_max, u + 1, 1, 0),
                        "max1_1": (turn_max, u + 1, 1, 1), "next_max0_0": (turn_max, u + 2, 0, 0),
                        "prev_normed1": (turn_normed, "prev_ctx1_1", "prev_ctx1_1"), "normed0": (turn_normed, "ctx0_1", "ctx0_1"),
                        "next_q0": (project_q, b + 1, 0), "next_q1": (project_q, b + 1, 1)}
                    if name[1] in "01" and name[0] in "qk":
                        h, g = int(name[-1]), int(name[1])
                        j = (turn_cols, u + 1 if g else u + 2, (q_cols if name[0] == "q" else k_cols)[g], h)
                    elif name.startswith("prev_hid") or name == "prev_router":
                        if name == "prev_router":
                            j = (route, [done("prev_hidT0"), done("prev_hidT1")])
                        elif "T" in name:
                            j = (turn_hidden, int(name[-1]), done(f"prev_hid{name[-1]}"))
                        else:
                            j = (hidden_half, int(name[-1]), done("prev_normed1"))
                    else:
                        j = job[name]
                        if j[0] is turn_normed:
                            j = (turn_normed, j[1], done(j[2]))
                    use(name, c, *j)

            def find_logits(u, g, two, i):
                h = 2 * two + i // 2
                if not is_int(u, 0) or two or i:
                    pe.wait_ge(logits_reduced, 8 * u + 4 * two + i)
                for k in range(2):
                    q = 2 * (i % 2) + k
                    last = nc.tensor.matmul(logit_bank[k][:, :], q_stack[g][0:K_MAX, h, q * P:(q + 1) * P],
                                            k_stack[g][0:K_MAX, h, :], start=True, stop=True)
                last.then_inc(logits_written, 1)

            def stack_ready(name, count):
                pe.wait_ge(emptied[BANK_OF[name]], count + 1)

            def head_and_block(j):
                two, k, h = j // (2 * NQ), (j // 2) % NQ, j % 2
                return two, k, 2 * two + h, h

            def find_keys(b, g, j):
                n = NJ * (2 * b + g) + j
                two, k, h, _ = head_and_block(j)
                if j == 2:
                    pe.wait_ge(vals_ready, 2 * b + g + 1)
                if j % (2 * NQ) == 0:
                    pe.wait_ge(max_loaded[g], 64 * b + 32 * (two + 1))
                if not (isinstance(n, int) and n < 2):
                    pe.wait_ge(probs_ready, n - 1)
                nc.tensor.matmul(key_bank[j % 2][:, :], k_stack[g][0:K_ALL, h, k * P:(k + 1) * P],
                                 q_stack[g][0:K_ALL, h, :], start=True, stop=True).then_inc(keys_written, 1)

            def weigh(u, g, j):
                n = NJ * u + j
                two, k, h, half = head_and_block(j)
                pe.wait_ge(probs_ready, n + 1)
                if k == 0 and half == 0:
                    if not (isinstance(u, int) and 2 * u + two < 2):
                        pe.wait_ge(ctx_copied, 2 * u + two - 1)
                nc.tensor.matmul(ctx_bank[two][half * 64:half * 64 + 64, :], vals[g][:, k, h, :],
                                 probsT[j % 4][:, :], start=(k == 0), stop=(k == NQ - 1)).then_inc(weighed, 1)

            pe.wait_ge(ident_ready, 1)
            for i, name in enumerate(("wqT", "woT")):
                pe.wait_ge(weights_loaded[i], 16)
                last = None
                for k in range(KD):
                    for m in range(KD):
                        c = k * D + m * P
                        last = turn(misc[BANK_OF[name]][:, c:c + P], w_nat[:, i, m, k * P:(k + 1) * P])
                last.then_inc(written[BANK_OF[name]], 1)
            pe.wait_ge(mask_loaded, 16)
            use("maskT", setup_count("maskT"), lambda m: turn(m[:, 0:B * NQ], mask_nat[:, :], B * NQ))
            pe.wait_ge(emptied[BANK_OF["wqT"]], 1)
            use("q0", setup_count("q0"), project_q, 0, 0)
            for name, _ in MISC_SETUP:
                if name.startswith("s0"):
                    use(name, setup_count(name), turn_cols, 0, (q_cols if name[2] == "q" else k_cols)[0], int(name[-1]))
                if name == "q1":
                    use(name, setup_count(name), project_q, 0, 1)
            for name, _ in MISC_SETUP:
                if name.startswith("s0"):
                    stack_ready(name, setup_count(name))
            for i in range(4):
                find_logits(0, 0, 0, i)
            use("max0", setup_count("max0"), turn_max, 0, 0, 0)
            pe.wait_ge(router_loaded, 16)
            pe.wait_ge(ones_ready, G)
            pe.wait_ge(emptied[BANK_OF["woT"]], setup_count("woT") + 1)

            def body(b, kind):
                for s in range(2 * NJ):
                    g, j = divmod(s, NJ)
                    u = 2 * b + g
                    last_unit = kind == LAST and g == 1
                    if j in (0, 2) and (kind != FIRST or g == 1):
                        h = 2 + j // 2
                        if g == 1:
                            for c in "kq":
                                stack_ready(f"{c}1_{h}", misc_count(b, kind, f"{c}1_{h}"))
                    if j in LOGIT_STEPS:
                        find_logits(u, g, 1, LOGIT_STEPS.index(j))
                    if j in (8, 10) and not last_unit:
                        h = (j - 8) // 2
                        for c in "kq":
                            name = f"{c}1_{h}" if g == 0 else f"{c}0_{h}"
                            stack_ready(name, misc_count(b, kind, name))
                    if j - 8 in LOGIT_STEPS and not last_unit:
                        find_logits(u + 1, 1 - g, 0, LOGIT_STEPS.index(j - 8))
                    find_keys(b, g, j)
                    if kind != FIRST or s >= 2:
                        if j >= 2:
                            weigh(u, g, j - 2)
                        else:
                            weigh(u - 1, 1 - g, j - 2 + NJ)
                    use_misc(b, kind, s)

            rows(pe, body)
            u = 2 * B - 1
            for j in (NJ - 2, NJ - 1):
                weigh(u, 1, j)
            use("tail_ctx1", tail("tail_ctx1"), turn_ctx, u, 1)
            use("tail_normed", tail("tail_normed"), turn_normed, "tail_ctx1", tail("tail_ctx1") + 1)
            for e in range(2):
                use(f"tail_hid{e}", tail(f"tail_hid{e}"), hidden_half, e, tail("tail_normed") + 1)
            for e in range(2):
                use(f"tail_hidT{e}", tail(f"tail_hidT{e}"), turn_hidden, e, tail(f"tail_hid{e}") + 1)
            use("tail_router", tail("tail_router"), route, [tail(f"tail_hidT{e}") + 1 for e in range(2)])

        @block.scalar
        def _(act):
            def empty(name, count, dst, view=lambda m: m[:, :]):
                i = BANK_OF[name]
                act.wait_ge(written[i], count + 1)
                nc.scalar.activation(dst, view(misc[i]), ACT.Copy).then_inc(emptied[i], 1)

            def empty_q(name, count, u):
                if not is_int(u, 0):
                    act.wait_ge(qm_ready, u)
                    act.wait_ge(vals_ready, u)
                empty(name, count, q_nat[:, :, :], four)

            def upper(u, g):
                act.wait_ge(qm_ready, u + 1)
                whole = qm[:, :, :].rearrange("p k (h d) -> p k h d", h=HPU)
                for cols, at in ((q_cols[g], 0), (q_cols[g], 2 * DK), (k_cols[g], 0), (k_cols[g], DK)):
                    nc.scalar.activation(cols[:, :, :, at:at + DK].bitcast(F32R), whole, ACT.Copy)\
                        .then_inc(hi_ready, 1)

            def empty_stack(name, count, stack, h):
                empty(name, count, stack[:, h, :])

            def upper_max(name, count, n):
                i = BANK_OF[name]
                act.wait_ge(written[i], count + 1)
                if not is_int(n, 0):
                    u2, g, two = max_place(n)
                    act.wait_ge(max_loaded[g], u2)
                nc.scalar.activation(max_hi[:, :], misc[i][0:2 * NQ, 0:P], ACT.Copy, scale=-1.0).then_inc(max_hi_ready, 1)

            def max_place(n):
                b, g, two = n
                return 64 * b + 32 * (two + 1), g, two

            def exp(n, j):
                act.wait_ge(keys_written, n + 1)
                if not (isinstance(n, int) and n < 4):
                    act.wait_ge(weighed, n - 3)
                nc.scalar.activation(probsT[j % 4][:, :], key_bank[j % 2][:, :], ACT.Exp, scale=SCALE)\
                    .then_inc(probs_ready, 1)

            def copy_ctx(u, two):
                act.wait_ge(weighed, NJ * u + 2 * NQ * (two + 1))
                nc.scalar.activation(ctx_raw[two][:, :], ctx_bank[two][:, :], ACT.Copy).then_inc(ctx_copied, 1)

            def empty_misc(b, kind, slot):
                for name, s, _ in misc_list(kind):
                    if s != slot:
                        continue
                    c = misc_count(b, kind, name)
                    if name in ("next_q0", "next_q1"):
                        empty_q(name, c, 2 * b + 2 + int(name[-1]))
                    elif name[0] == "k":
                        empty_stack(name, c, k_stack[int(name[1])], int(name[-1]))
                    elif name == "prev_normed1":
                        empty(name, c, ctxn[:, 1, :])
                    elif name == "normed0":
                        empty(name, c, ctxn[:, 0, :])
                    elif name == "prev_hid0":
                        act.wait_ge(hidden_stored, 16 * b)
                        empty(name, c, hid[:, 0, :])
                    elif name == "prev_hidT0":
                        empty(name, c, hidT[:, 0, :, :], four)
                    elif name == "max0_1":
                        upper_max(name, c, (b, 0, 0))
                    elif name == "max1_0":
                        upper_max(name, c, (b, 0, 1))
                    elif name == "max1_1":
                        upper_max(name, c, (b, 1, 0))
                    elif name == "next_max0_0":
                        upper_max(name, c, (b, 1, 1))

            empty("wqT", 0, wqT[:, :, :], lambda m: m[:, :].rearrange("p (k c) -> p k c", k=KD))
            empty("woT", 0, woT[:, :, :], lambda m: m[:, :].rearrange("p (k c) -> p k c", k=KD))
            empty("maskT", setup_count("maskT"), mask_cols[:, :], lambda m: m[:, 0:B * NQ])
            empty_q("q0", setup_count("q0"), 0)
            upper(0, 0)
            for name, _ in MISC_SETUP:
                if name.startswith("s0k"):
                    empty_stack(name, setup_count(name), k_stack[0], int(name[-1]))
            empty_q("q1", setup_count("q1"), 1)
            upper(1, 1)
            upper_max("max0", setup_count("max0"), 0)

            def body(b, kind):
                for s in range(2 * NJ):
                    g, j = divmod(s, NJ)
                    exp(NJ * (2 * b + g) + j, j)
                    if j == 1 and (kind != FIRST or g == 1):
                        copy_ctx(2 * b + g - 1, 1)
                    if j == 2 * NQ + 1:
                        copy_ctx(2 * b + g, 0)
                    empty_misc(b, kind, s)
                    if j == 7 and kind != LAST:
                        upper(2 * b + 2 + g, g)

            rows(act, body)
            copy_ctx(2 * B - 1, 1)
            empty("tail_normed", tail("tail_normed"), ctxn[:, 1, :])
            act.wait_ge(hidden_stored, 16 * B)
            empty("tail_hid0", tail("tail_hid0"), hid[:, 0, :])
            empty("tail_hidT0", tail("tail_hidT0"), hidT[:, 0, :, :], four)

        @block.vector
        def _(dve):
            def empty(name, count, dst, view=lambda m: m[:, :]):
                i = BANK_OF[name]
                dve.wait_ge(written[i], count + 1)
                nc.vector.tensor_copy(dst, view(misc[i])).then_inc(emptied[i], 1)

            def reduce(u, g, two, i):
                dve.wait_ge(logits_written, 8 * u + 4 * two + i + 1)
                c = 2 * NQ * two + 2 * i
                nc.vector.tensor_reduce(row_max[g][:, c:c + 2], first_banks[:, :, :], AX.X, ALU.max).then_inc(logits_reduced, 1)

            def lower_max(name, count, n):
                i = BANK_OF[name]
                dve.wait_ge(max_hi_ready, n + 1)
                nc.vector.scalar_tensor_tensor(out=max_lo[:, :], in0=misc[i][0:2 * NQ, 0:P], scalar=-1.0,
                                               in1=max_hi[:, :].bitcast(F32), op0=ALU.mult, op1=ALU.subtract)\
                    .then_inc(emptied[i], 1)

            def normalise(name, count, u, two):
                i = BANK_OF[name]
                n = 2 * u + two
                v = misc[i][:, :].rearrange("p (k h c) -> p k h c", k=NQ, h=2)
                dve.wait_ge(written[i], count + 1)
                nc.vector.reciprocal(inv_sum[two][:, :, :], v[:, :, :, DK]).then_inc(inv_ready, 1)
                dve.wait_ge(inv_ready, n + 1)
                nc.vector.tensor_tensor(ctx_nat[:, :, 2 * two:2 * two + 2, :], v[:, :, :, 0:DK],
                                        inv_sum[two][:, :, :].unsqueeze(3).broadcast_to([P, NQ, 2, DK]), ALU.mult)\
                    .then_inc(emptied[i], 1)

            def empty_misc(b, kind, slot):
                for name, s, _ in misc_list(kind):
                    if s != slot:
                        continue
                    c = misc_count(b, kind, name)
                    if name[0] == "q":
                        empty(name, c, q_stack[int(name[1])][:, int(name[-1]), :])
                    elif name == "prev_hid1":
                        dve.wait_ge(hidden_stored, 16 * b)
                        empty(name, c, hid[:, 1, :])
                    elif name == "prev_hidT1":
                        empty(name, c, hidT[:, 1, :, :], four)
                    elif name == "prev_router":
                        empty(name, c, logits_all[:, bass.ds((b - 1) * KD, KD), :],
                              lambda m: m[:, 0:KD * E].rearrange("p (k e) -> p k e", k=KD))
                    elif name == "max0_1":
                        lower_max(name, c, 4 * b + 1)
                    elif name == "max1_0":
                        lower_max(name, c, 4 * b + 2)
                    elif name == "max1_1":
                        lower_max(name, c, 4 * b + 3)
                    elif name == "next_max0_0":
                        lower_max(name, c, 4 * b + 4)
                    elif name == "prev_ctx1_1":
                        normalise(name, c, 2 * b - 1, 1)
                    elif name == "ctx0_0":
                        normalise(name, c, 2 * b, 0)
                    elif name == "ctx0_1":
                        normalise(name, c, 2 * b, 1)
                    elif name == "ctx1_0":
                        normalise(name, c, 2 * b + 1, 0)

            for g in range(G):
                nc.vector.memset(k_cols[g][:, :, :, R_MAX:P], 1.0).then_inc(cols_cleared, 1)
                nc.vector.memset(q_cols[g][:, :, :, R_MAX:P], 0.0).then_inc(cols_cleared, 1)
                nc.vector.memset(vals[g][:, :, :, DK:2 * DK], 1.0).then_inc(ones_ready, 1)
            for name, _ in MISC_SETUP:
                if name.startswith("s0q"):
                    empty(name, setup_count(name), q_stack[0][:, int(name[-1]), :])
            for i in range(4):
                reduce(0, 0, 0, i)
            lower_max("max0", setup_count("max0"), 0)

            def body(b, kind):
                for s in range(2 * NJ):
                    g, j = divmod(s, NJ)
                    u = 2 * b + g
                    if j in LOGIT_STEPS:
                        reduce(u, g, 1, LOGIT_STEPS.index(j))
                    if j - 8 in LOGIT_STEPS and not (kind == LAST and g == 1):
                        reduce(u + 1, 1 - g, 0, LOGIT_STEPS.index(j - 8))
                    empty_misc(b, kind, s)

            rows(dve, body)
            normalise("tail_ctx1", tail("tail_ctx1"), 2 * B - 1, 1)
            dve.wait_ge(hidden_stored, 16 * B)
            empty("tail_hid1", tail("tail_hid1"), hid[:, 1, :])
            empty("tail_hidT1", tail("tail_hidT1"), hidT[:, 1, :, :], four)
            empty("tail_router", tail("tail_router"), logits_all[:, (B - 1) * KD:B * KD, :],
                  lambda m: m[:, 0:KD * E].rearrange("p (k e) -> p k e", k=KD))


        attention.close()

        NT = -(-(2 * TOKENS + E * (P - 1)) // (2 * P)) * 2
        KI = I // P

        def sb(name, shape, dt=F32):
            return ctx.enter_context(nc.sbuf_tensor(name, shape, dt))

        gate_up_sb = sb("gate_up_sb", [P, E * KT, F2])
        down_sb = sb("down_sb", [P, E * KI, T])
        experts_loaded = sem("experts_loaded")
        slot_token = sb("slot_token", [P, NT], I32)
        slot_prob = sb("slot_prob", [P, NT])
        tile_expert = sb("tile_expert", [1, NT], I32)
        token_slot = sb("token_slot", [P, 2, TT], I32)
        expert_rows = nc.dram_tensor("expert_rows_dram", [NT * P, T], F32)

        routing = ExitStack()
        ctx.enter_context(routing)
        with routing:
            def rb(name, shape, dt=F32):
                return routing.enter_context(nc.sbuf_tensor(name, shape, dt))

            expert_no = rb("expert_no", [P, TT, E])
            before_e = rb("before_e", [P, E, E])
            tile_no = rb("tile_no", [P, NT])
            place_no = rb("place_no", [P, P])
            token_no = rb("token_no", [P, TT])
            place_i = rb("place_i", [P, P], I32)
            earlier = rb("earlier", [P, P])
            ones = rb("ones", [P, P])
            best = rb("best", [P, 2, TT])
            chosen = [rb(f"chosen{c}", [P, TT, E]) for c in range(2)]
            rest = rb("rest", [P, TT, E])
            cand = rb("cand", [P, TT, E])
            cand_min = rb("cand_min", [P, TT])
            both = rb("both", [P, TT, E])
            sigm = rb("sigm", [P, 2, TT])
            prob = rb("prob", [P, 2, TT])
            totals = rb("totals", [P, TT, E])
            cum = [rb(f"cum{i}", [P, TT, E]) for i in range(2)]
            slots = rb("slots", [P, TT, E])
            over = rb("over", [P, E, TT])
            tiles_of = rb("tiles_of", [P, E])
            pairs = rb("pairs", [P, E, E])
            first_tile = rb("first_tile", [P, E])
            end_tile = rb("end_tile", [P, E])
            passed = rb("passed", [P, NT, E - 1])
            expert_f = rb("expert_f", [P, NT])
            slot_f = rb("slot_f", [P, 2, TT])
            slot_i = rb("slot_i", [P, 2, TT], I32)
            s_tile_i = rb("s_tile_i", [P, 2, TT], I32)
            s_place_i = rb("s_place_i", [P, 2, TT], I32)
            s_tile = rb("s_tile", [P, 2, TT])
            s_place = rb("s_place", [P, 2, TT])
            at_place = [rb(f"at_place{i}", [P, P]) for i in range(2)]
            at_tile = [rb(f"at_tile{i}", [P, 2, NT]) for i in range(2)]

            def rsem(name):
                return routing.enter_context(nc.semaphore(name))

            constants_ready = rsem("constants_ready")
            chain = rsem("chain")
            best_ready = rsem("best_ready")
            sigm_ready = rsem("sigm_ready")
            both_ready = rsem("both_ready")
            counted = rsem("counted")
            pair_ready = rsem("pair_ready")
            pair_added = rsem("pair_added")
            block2 = routing.enter_context(nc.Block())

            @block2.sync
            def _(sp):
                for e in range(E):
                    sp.dma_start(gate_up_sb[:, e * KT:(e + 1) * KT, :],
                                 gate_up_w[e].rearrange("(k p) f -> p k f", p=P)).then_inc(experts_loaded, 16)
                    sp.dma_start(down_sb[:, e * KI:(e + 1) * KI, :],
                                 down_w[e].rearrange("(k p) d -> p k d", p=P)).then_inc(experts_loaded, 16)

            @block2.gpsimd
            def _(pool):
                kw = dict(allow_small_or_imprecise_dtypes=True)
                nc.gpsimd.iota(expert_no[:, :, :], [[0, TT], [1, E]], base=0, channel_multiplier=0, **kw)
                nc.gpsimd.iota(tile_no[:, :], [[1, NT]], base=0, channel_multiplier=0, **kw)
                nc.gpsimd.iota(place_no[:, :], [[1, P]], base=0, channel_multiplier=0, **kw)
                nc.gpsimd.iota(token_no[:, :], [[P, TT]], base=0, channel_multiplier=1, **kw)
                nc.gpsimd.memset(ones[:, :], 1.0).then_inc(constants_ready, 1)
                nc.gpsimd.memset(before_e[:, :, :], 1.0).then_inc(constants_ready, 1)
                pool.wait_ge(constants_ready, 2)
                nc.gpsimd.affine_select(out=earlier[:, :], in_=ones[:, :], compare_op=ALU.is_gt, fill=0.0,
                                        base=0, pattern=[[1, P]], channel_multiplier=-1)
                nc.gpsimd.affine_select(out=before_e[:, :, :], in_=before_e[:, :, :], compare_op=ALU.is_gt, fill=0.0,
                                        base=0, pattern=[[1, E], [-1, E]], channel_multiplier=0)\
                    .then_inc(constants_ready, 1)

            @block2.scalar
            def _(act):
                act.wait_ge(best_ready, 1)
                nc.scalar.activation(sigm[:, :, :], best[:, :, :], ACT.Exp, scale=-1.0).then_inc(sigm_ready, 1)

            @block2.tensor
            def _(pe):
                pe.wait_ge(constants_ready, 3)
                pe.wait_ge(both_ready, 1)
                flat = both[:, :, :].rearrange("p t e -> p (t e)")
                nc.tensor.matmul(bank[0][:, 0:TT * E], earlier[:, :], flat, start=True, stop=True)
                nc.tensor.matmul(bank[1][:, 0:TT * E], ones[:, :], flat, start=True, stop=True).then_inc(counted, 1)
                for n in range(2 * TT):
                    pe.wait_ge(pair_ready, n + 1)
                    nc.tensor.matmul(bank[2][:, 0:2 * NT], at_place[n % 2][:, :],
                                     at_tile[n % 2][:, :, :].rearrange("p a b -> p (a b)"),
                                     start=(n == 0), stop=(n == 2 * TT - 1)).then_inc(pair_added, 1)

            @block2.vector
            def _(dve):
                done = [0]

                def link(ins):
                    done[0] += 1
                    ins.then_inc(chain, 1)
                    dve.wait_ge(chain, done[0])

                v = nc.vector
                wide = [P, TT, E]
                dve.wait_ge(constants_ready, 3)
                src = logits_all
                for c in range(2):
                    link(v.tensor_reduce(best[:, c, :], src[:, :, :], AX.X, ALU.max))
                    link(v.tensor_tensor(cand[:, :, :], src[:, :, :], best[:, c, :].unsqueeze(2).broadcast_to(wide),
                                         ALU.is_equal))
                    link(v.scalar_tensor_tensor(out=cand[:, :, :], in0=cand[:, :, :], scalar=-float(E),
                                                in1=expert_no[:, :, :], op0=ALU.mult, op1=ALU.add))
                    link(v.tensor_reduce(cand_min[:, :], cand[:, :, :], AX.X, ALU.min))
                    link(v.tensor_tensor(chosen[c][:, :, :], cand[:, :, :],
                                         cand_min[:, :].unsqueeze(2).broadcast_to(wide), ALU.is_equal))
                    if c == 0:
                        link(v.scalar_tensor_tensor(out=rest[:, :, :], in0=chosen[0][:, :, :], scalar=LOWEST,
                                                    in1=logits_all[:, :, :], op0=ALU.mult, op1=ALU.add))
                        src = rest
                v.tensor_tensor(both[:, :, :], chosen[0][:, :, :], chosen[1][:, :, :], ALU.add).then_inc(both_ready, 1)
                v.tensor_copy(cand_min[:, :], best[:, 1, :]).then_inc(best_ready, 1)
                dve.wait_ge(sigm_ready, 1)
                link(v.tensor_scalar(sigm[:, :, :], sigm[:, :, :], 1.0, None, ALU.add))
                link(v.reciprocal(prob[:, :, :], sigm[:, :, :]))
                dve.wait_ge(counted, 1)
                link(v.tensor_copy(totals[:, :, :], bank[1][:, 0:TT * E].rearrange("p (t e) -> p t e", e=E)))
                src, step, i = totals, 1, 0
                while step < TT:
                    v.tensor_copy(cum[i][:, 0:step, :], src[:, 0:step, :])
                    link(v.tensor_tensor(cum[i][:, step:TT, :], src[:, step:TT, :], src[:, 0:TT - step, :], ALU.add))
                    src, step, i = cum[i], 2 * step, 1 - i
                inclusive, spare = src, cum[i]
                link(v.tensor_tensor(spare[:, :, :], inclusive[:, :, :], totals[:, :, :], ALU.subtract))
                link(v.tensor_tensor(slots[:, :, :], spare[:, :, :],
                                     bank[0][:, 0:TT * E].rearrange("p (t e) -> p t e", e=E), ALU.add))
                link(v.tensor_scalar(rest[:, 0, :], inclusive[:, TT - 1, :], 1.0 / P, None, ALU.mult))
                link(v.tensor_tensor(over[:, :, :], rest[:, 0, :].unsqueeze(2).broadcast_to([P, E, TT]),
                                     tile_no[:, 0:TT].unsqueeze(1).broadcast_to([P, E, TT]), ALU.is_gt))
                link(v.tensor_reduce(tiles_of[:, :], over[:, :, :], AX.X, ALU.add))
                link(v.tensor_tensor(pairs[:, :, :], before_e[:, :, :],
                                     tiles_of[:, :].unsqueeze(1).broadcast_to([P, E, E]), ALU.mult))
                link(v.tensor_reduce(first_tile[:, :], pairs[:, :, :], AX.X, ALU.add))
                link(v.tensor_tensor(end_tile[:, :], first_tile[:, :], tiles_of[:, :], ALU.add))
                link(v.tensor_tensor(passed[:, :, :], end_tile[:, 0:E - 1].unsqueeze(1).broadcast_to([P, NT, E - 1]),
                                     tile_no[:, :].unsqueeze(2).broadcast_to([P, NT, E - 1]), ALU.is_le))
                link(v.tensor_reduce(expert_f[:, :], passed[:, :, :], AX.X, ALU.add))
                v.tensor_copy(tile_expert[:, :], expert_f[0:1, :])
                link(v.scalar_tensor_tensor(out=slots[:, :, :],
                                            in0=first_tile[:, :].unsqueeze(1).broadcast_to(wide), scalar=float(P),
                                            in1=slots[:, :, :], op0=ALU.mult, op1=ALU.add))
                for c in range(2):
                    link(v.tensor_tensor(cand[:, :, :], chosen[c][:, :, :], slots[:, :, :], ALU.mult))
                    link(v.tensor_reduce(slot_f[:, c, :], cand[:, :, :], AX.X, ALU.add))
                v.tensor_copy(token_slot[:, :, :], slot_f[:, :, :])
                link(v.tensor_copy(slot_i[:, :, :], slot_f[:, :, :]))
                v.tensor_scalar(s_tile_i[:, :, :], slot_i[:, :, :], P.bit_length() - 1, None, ALU.logical_shift_right)
                link(v.tensor_scalar(s_place_i[:, :, :], slot_i[:, :, :], P - 1, None, ALU.bitwise_and))
                v.tensor_copy(s_tile[:, :, :], s_tile_i[:, :, :])
                link(v.tensor_copy(s_place[:, :, :], s_place_i[:, :, :]))
                for n in range(2 * TT):
                    c, t = divmod(n, TT)
                    if n >= 2:
                        dve.wait_ge(pair_added, n - 1)
                    v.tensor_scalar(at_place[n % 2][:, :], place_no[:, :], s_place[:, c, t:t + 1], None, ALU.is_equal)
                    v.tensor_scalar(at_tile[n % 2][:, 0, :], tile_no[:, :], s_tile[:, c, t:t + 1],
                                    token_no[:, t:t + 1], ALU.is_equal, ALU.mult)
                    v.tensor_scalar(at_tile[n % 2][:, 1, :], tile_no[:, :], s_tile[:, c, t:t + 1],
                                    prob[:, c, t:t + 1], ALU.is_equal, ALU.mult).then_inc(pair_ready, 1)
                dve.wait_ge(pair_added, 2 * TT)
                v.tensor_copy(slot_token[:, :], bank[2][:, 0:NT])
                v.tensor_copy(slot_prob[:, :], bank[2][:, NT:2 * NT])

        experts = ExitStack()
        ctx.enter_context(experts)
        with experts:
            def eb(name, shape, dt=F32):
                return [experts.enter_context(nc.sbuf_tensor(f"{name}{i}", shape, dt)) for i in range(2)]

            def esem(name):
                return experts.enter_context(nc.semaphore(name))

            row_no = eb("row_no", [P, 1], I32)
            row_prob = eb("row_prob", [P, 1])
            rows_in = eb("rows_in", [P, T])
            rows_scaled = eb("rows_scaled", [P, T])
            rows_T = eb("rows_T", [P, KT, P])
            gated = eb("gated", [P, I])
            act_h = eb("act_h", [P, I])
            act_hT = eb("act_hT", [P, KI, P])
            rows_out = eb("rows_out", [P, T])
            inT_bank, gu_bank, hT_bank, out_bank = bank[0:2], bank[2:4], bank[4:6], bank[6:8]

            gathered = [esem(f"gathered{i}") for i in range(2)]
            row_no_ready = esem("row_no_ready")
            scaled = esem("scaled")
            in_turned = esem("in_turned")
            in_copied = esem("in_copied")
            gu_done = esem("gu_done")
            silu_done = esem("silu_done")
            h_done = esem("h_done")
            h_turned = esem("h_turned")
            h_copied = esem("h_copied")
            down_done = esem("down_done")
            out_copied = esem("out_copied")
            stored = [esem(f"stored{i}") for i in range(2)]
            block3 = experts.enter_context(nc.Block())

            def tiles(eng, step):
                for n in range(4):
                    step(n, n % 2)
                with eng.Fori(2, NT // 2 - 1) as n:
                    for i in range(2):
                        step(2 * n + i, i)
                for n in range(NT - 2, NT + 1):
                    step(n, n % 2)

            def first(n):
                return isinstance(n, int) and n < 2

            def exists(n):
                return not isinstance(n, int) or 0 <= n < NT

            @block3.gpsimd
            def _(pool):
                def step(n, i):
                    if not exists(n):
                        return
                    if not first(n):
                        pool.wait_ge(scaled, n - 1)
                    nc.gpsimd.tensor_copy(row_prob[i][:, :], slot_prob[:, bass.ds(n, 1)])
                    nc.gpsimd.tensor_copy(row_no[i][:, :], slot_token[:, bass.ds(n, 1)]).then_inc(row_no_ready, 1)
                    pool.wait_ge(row_no_ready, n + 1)
                    pool.sem_inc(pool_waits_passed, 1)
                    nc.gpsimd.indirect_dma_start(rows_in[i][:, :], None, hidden[:, :],
                                                 bass.IndirectOffsetOnAxis(ap=row_no[i][:, 0:1], axis=0))\
                        .then_inc(gathered[i], 16)
                tiles(pool, step)

            @block3.vector
            def _(dve):
                def scale_rows(n, i):
                    dve.wait_ge(gathered[i], 8 * (n - i) + 16)
                    if not first(n):
                        dve.wait_ge(in_turned, n - 1)
                    nc.vector.tensor_scalar(rows_scaled[i][:, :], rows_in[i][:, :], row_prob[i][:, 0:1], None, ALU.mult)\
                        .then_inc(scaled, 1)

                def combine(n, i):
                    dve.wait_ge(silu_done, n + 1)
                    if not first(n):
                        dve.wait_ge(h_turned, n - 1)
                    nc.vector.tensor_tensor(act_h[i][:, :], gated[i][:, :], gu_bank[i][:, I:F2], ALU.mult)\
                        .then_inc(h_done, 1)

                def copy_h(n, i):
                    dve.wait_ge(h_turned, n + 1)
                    if not first(n):
                        dve.wait_ge(down_done, n - 1)
                    nc.vector.tensor_copy(act_hT[i][:, :, :],
                                          hT_bank[i][:, 0:I].rearrange("p (k c) -> p k c", k=KI)).then_inc(h_copied, 1)

                def step(n, i):
                    if exists(n - 1):
                        copy_h(n - 1, 1 - i)
                    if exists(n):
                        combine(n, i)
                    if exists(n + 2):
                        scale_rows(n + 2, i)
                for n in range(2):
                    scale_rows(n, n)
                tiles(dve, step)

            @block3.scalar
            def _(act):
                def copy_in(n, i):
                    act.wait_ge(in_turned, n + 1)
                    if not first(n):
                        act.wait_ge(gu_done, n - 1)
                    nc.scalar.activation(rows_T[i][:, :, :], inT_bank[i][:, :].rearrange("p (k c) -> p k c", k=KT),
                                         ACT.Copy).then_inc(in_copied, 1)

                def silu(n, i):
                    act.wait_ge(gu_done, n + 1)
                    if not first(n):
                        act.wait_ge(h_done, n - 1)
                    nc.scalar.activation(gated[i][:, :], gu_bank[i][:, 0:I], ACT.Silu).then_inc(silu_done, 1)

                def copy_out(n, i):
                    act.wait_ge(down_done, n + 1)
                    if not first(n):
                        act.wait_ge(stored[i], 8 * (n - i))
                    nc.scalar.activation(rows_out[i][:, :], out_bank[i][:, :], ACT.Copy).then_inc(out_copied, 1)

                def step(n, i):
                    if exists(n):
                        silu(n, i)
                    if exists(n + 1):
                        copy_in(n + 1, 1 - i)
                    if exists(n - 1):
                        copy_out(n - 1, 1 - i)
                copy_in(0, 0)
                tiles(act, step)

            @block3.sync
            def _(sp):
                def step(n, i):
                    if exists(n - 1):
                        sp.wait_ge(out_copied, n)
                        sp.sem_inc(sp_waits_passed, 1)
                        sp.dma_start(expert_rows[bass.ds((n - 1) * P, P), :], rows_out[1 - i][:, :])\
                            .then_inc(stored[1 - i], 16)
                tiles(sp, step)
                for i in range(2):
                    sp.wait_ge(stored[i], 8 * NT)

            @block3.tensor
            def _(pe):
                pe.wait_ge(experts_loaded, 2 * E * 16)

                def expert(n):
                    return pe.value_load(tile_expert[0:1, bass.ds(n, 1)], min_val=0, max_val=E - 1)

                def turn_in(n, i):
                    pe.wait_ge(scaled, n + 1)
                    if not first(n):
                        pe.wait_ge(in_copied, n - 1)
                    for k in range(KT):
                        last = nc.tensor.transpose(inT_bank[i][:, k * P:(k + 1) * P],
                                                   rows_scaled[i][:, k * P:(k + 1) * P], ident[:, :])
                    last.then_inc(in_turned, 1)

                def gate_up(n, i, e):
                    pe.wait_ge(in_copied, n + 1)
                    if not first(n):
                        pe.wait_ge(h_done, n - 1)
                    for k in range(KT):
                        w = gate_up_sb[:, bass.ds(e * KT + k, 1), :].rearrange("p o f -> p (o f)")
                        last = nc.tensor.matmul(gu_bank[i][:, :], rows_T[i][:, k, :], w,
                                                start=(k == 0), stop=(k == KT - 1))
                    last.then_inc(gu_done, 1)

                def turn_h(n, i):
                    pe.wait_ge(h_done, n + 1)
                    if not first(n):
                        pe.wait_ge(h_copied, n - 1)
                    for k in range(KI):
                        last = nc.tensor.transpose(hT_bank[i][:, k * P:(k + 1) * P],
                                                   act_h[i][:, k * P:(k + 1) * P], ident[:, :])
                    last.then_inc(h_turned, 1)

                def down(n, i, e):
                    pe.wait_ge(h_copied, n + 1)
                    if not first(n):
                        pe.wait_ge(out_copied, n - 1)
                    for k in range(KI):
                        w = down_sb[:, bass.ds(e * KI + k, 1), :].rearrange("p o f -> p (o f)")
                        last = nc.tensor.matmul(out_bank[i][:, :], act_hT[i][:, k, :], w,
                                                start=(k == 0), stop=(k == KI - 1))
                    last.then_inc(down_done, 1)

                def step(n, i):
                    if exists(n):
                        gate_up(n, i, expert(n))
                    if exists(n - 1):
                        e = expert(n - 1)
                        turn_h(n - 1, 1 - i)
                    if exists(n + 1):
                        turn_in(n + 1, 1 - i)
                    if exists(n - 1):
                        down(n - 1, 1 - i, e)
                turn_in(0, 0)
                tiles(pe, step)

        shared = ExitStack()
        ctx.enter_context(shared)
        with shared:
            def fb(name, shape, dt=F32):
                return [shared.enter_context(nc.sbuf_tensor(f"{name}{i}", shape, dt)) for i in range(2)]

            def fsem(name):
                return shared.enter_context(nc.semaphore(name))

            tok = fb("tok", [P, KD, T])
            x_in = fb("x_in", [P, KD, T])
            tokT = fb("tokT", [P, KT, D])
            sgate = fb("sgate", [P, KI, D])
            sh = fb("sh", [P, KI, D])
            slot_no = [fb(f"slot_no{c}_", [P, 1], I32) for c in range(2)]
            expert_row = [fb(f"expert_row{c}_", [P, T]) for c in range(2)]
            total = fb("total", [P, T])
            gate_bank, up_bank, sum_bank = (bank[2], bank[4]), (bank[3], bank[5]), bank[6:8]

            tok_loaded = [fsem(f"tok_loaded{i}") for i in range(2)]
            x_in_loaded = [fsem(f"x_in_loaded{i}") for i in range(2)]
            tok_turned = fsem("tok_turned")
            tokT_copied = fsem("tokT_copied")
            up_done = fsem("up_done")
            sgate_done = fsem("sgate_done")
            sh_done = fsem("sh_done")
            shared_done = fsem("shared_done")
            slot_no_ready = fsem("slot_no_ready")
            row_gathered = [fsem(f"row_gathered{i}") for i in range(2)]
            row_sum_ready = fsem("row_sum_ready")
            x_added = fsem("x_added")
            total_ready = fsem("total_ready")
            out_stored = [fsem(f"out_stored{i}") for i in range(2)]
            block4 = shared.enter_context(nc.Block())

            def row_steps(eng, step):
                for b in range(4):
                    step(b, b % 2)
                with eng.Fori(2, B // 2 - 1) as n:
                    for i in range(2):
                        step(2 * n + i, i)
                for b in range(B - 2, B + 1):
                    step(b, b % 2)

            def first_rows(b, n=2):
                return isinstance(b, int) and b < n

            def is_row(b):
                return not isinstance(b, int) or 0 <= b < B

            out_rows = out.rearrange("b d t -> (b d) t")

            @block4.sync
            def _(sp):
                def load(b, i):
                    if not first_rows(b):
                        sp.wait_ge(tok_turned, 2 * (b - 1))
                        sp.sem_inc(sp_waits_passed, 1)
                    sp.dma_start(tok[i][:, :, :], hidden[bass.ds(b * D, D), :].rearrange("(k p) t -> p k t", p=P))\
                        .then_inc(tok_loaded[i], 16)

                def load_x(b, i):
                    if not first_rows(b):
                        sp.wait_ge(x_added, 2 * (b - 1))
                        sp.sem_inc(sp_waits_passed, 1)
                    sp.dma_start(x_in[i][:, :, :], x[bass.ds(b, 1)].rearrange("o (k p) t -> p (o k) t", p=P))\
                        .then_inc(x_in_loaded[i], 16)

                def step(b, i):
                    if is_row(b):
                        load_x(b, i)
                    if is_row(b + 2):
                        load(b + 2, i)
                load(0, 0)
                load(1, 1)
                row_steps(sp, step)

            @block4.scalar
            def _(act):
                def copy_tokens(b, i):
                    for h in range(2):
                        act.wait_ge(tok_turned, 2 * b + h + 1)
                        if h == 0 and not first_rows(b):
                            act.wait_ge(up_done, b - 1)
                        nc.scalar.activation(tokT[i][:, 2 * h:2 * h + 2, :],
                                             bank[h][:, :].rearrange("p (k c) -> p k c", k=2), ACT.Copy)\
                            .then_inc(tokT_copied, 1)

                def silu(b, i):
                    act.wait_ge(up_done, b + 1)
                    if not first_rows(b):
                        act.wait_ge(sh_done, b - 1)
                    nc.scalar.activation(sgate[i][:, :, :], gate_bank[i][:, :].rearrange("p (k c) -> p k c", k=KI),
                                         ACT.Silu).then_inc(sgate_done, 1)

                def store(b):
                    for h in range(KD):
                        act.wait_ge(total_ready, 2 * b + h + 1)
                        act.dma_start(out_rows[bass.ds((2 * b + h) * P, P), :], total[h][:, :])\
                            .then_inc(out_stored[h], 16)

                def step(b, i):
                    if is_row(b):
                        silu(b, i)
                    if is_row(b + 1):
                        copy_tokens(b + 1, 1 - i)
                    if is_row(b - 1):
                        store(b - 1)
                copy_tokens(0, 0)
                row_steps(act, step)
                for h in range(KD):
                    act.wait_ge(out_stored[h], 16 * B)

            @block4.tensor
            def _(pe):
                pe.wait_ge(shared_loaded, 48)

                def turn_tokens(b, i):
                    pe.wait_ge(tok_loaded[i], 8 * (b - i) + 16)
                    for h in range(2):
                        if not first_rows(b, 1):
                            pe.wait_ge(tokT_copied, 2 * b - 1 + h)
                        for k in range(2):
                            for m in range(KD):
                                c = k * D + m * P
                                last = nc.tensor.transpose(bank[h][:, c:c + P],
                                                           tok[i][:, m, (2 * h + k) * P:(2 * h + k + 1) * P], ident[:, :])
                        last.then_inc(tok_turned, 1)

                def gate_up(b, i):
                    pe.wait_ge(tokT_copied, 2 * b + 2)
                    if not first_rows(b):
                        pe.wait_ge(sh_done, b - 1)
                    for w, dst in zip(shared_in, (gate_bank[i], up_bank[i])):
                        for m in range(KI):
                            for k in range(KT):
                                last = nc.tensor.matmul(dst[:, m * D:(m + 1) * D], w[:, k, m * P:(m + 1) * P],
                                                        tokT[i][:, k, :], start=(k == 0), stop=(k == KT - 1))
                    last.then_inc(up_done, 1)

                def down(b, i):
                    pe.wait_ge(sh_done, b + 1)
                    for h in range(KD):
                        if not first_rows(b, 1):
                            pe.wait_ge(total_ready, 2 * b - 1 + h)
                        for k in range(KI):
                            last = nc.tensor.matmul(sum_bank[h][:, :], sh[i][:, k, h * P:(h + 1) * P],
                                                    shared_out[:, k, :], start=(k == 0), stop=(k == KI - 1))
                        last.then_inc(shared_done, 1)

                def step(b, i):
                    if is_row(b):
                        gate_up(b, i)
                    if is_row(b + 1):
                        turn_tokens(b + 1, 1 - i)
                    if is_row(b - 1):
                        down(b - 1, 1 - i)
                turn_tokens(0, 0)
                row_steps(pe, step)

            @block4.gpsimd
            def _(pool):
                def step(b, i):
                    if not is_row(b):
                        return
                    for h in range(KD):
                        n = 2 * b + h
                        if not first_rows(b, 1):
                            pool.wait_ge(total_ready, n - 1)
                        for c in range(2):
                            nc.gpsimd.tensor_copy(slot_no[c][h][:, :], token_slot[:, c, bass.ds(n, 1)])\
                                .then_inc(slot_no_ready, 1)
                        pool.wait_ge(slot_no_ready, 2 * n + 2)
                        pool.sem_inc(pool_waits_passed, 1)
                        for c in range(2):
                            nc.gpsimd.indirect_dma_start(expert_row[c][h][:, :], None, expert_rows[:, :],
                                                         bass.IndirectOffsetOnAxis(ap=slot_no[c][h][:, 0:1], axis=0))\
                                .then_inc(row_gathered[h], 16)
                row_steps(pool, step)

            @block4.vector
            def _(dve):
                def combine(b, i):
                    dve.wait_ge(sgate_done, b + 1)
                    if not first_rows(b):
                        dve.wait_ge(shared_done, 2 * (b - 1))
                    nc.vector.tensor_tensor(sh[i][:, :, :], sgate[i][:, :, :],
                                            up_bank[i][:, :].rearrange("p (k c) -> p k c", k=KI), ALU.mult)\
                        .then_inc(sh_done, 1)

                def add_up(b, i):
                    for h in range(KD):
                        dve.wait_ge(row_gathered[h], 32 * (b + 1))
                        nc.vector.tensor_tensor(expert_row[0][h][:, :], expert_row[0][h][:, :], expert_row[1][h][:, :],
                                                ALU.add).then_inc(row_sum_ready, 1)
                    dve.wait_ge(x_in_loaded[i], 8 * (b - i) + 16)
                    for h in range(KD):
                        dve.wait_ge(row_sum_ready, 2 * b + h + 1)
                        nc.vector.tensor_tensor(expert_row[0][h][:, :], expert_row[0][h][:, :], x_in[i][:, h, :], ALU.add)\
                            .then_inc(x_added, 1)
                    for h in range(KD):
                        n = 2 * b + h
                        dve.wait_ge(x_added, n + 1)
                        dve.wait_ge(shared_done, n + 1)
                        if not first_rows(b, 1):
                            dve.wait_ge(out_stored[h], 16 * b)
                        nc.vector.tensor_tensor(total[h][:, :], sum_bank[h][:, :], expert_row[0][h][:, :], ALU.add)\
                            .then_inc(total_ready, 1)

                def step(b, i):
                    if is_row(b):
                        combine(b, i)
                    if is_row(b - 1):
                        add_up(b - 1, 1 - i)
                row_steps(dve, step)



_INS = ["x", "cond_2048", "L0_cond_Wq", "L0_cond_Wo", "L0_ffn_router_w", "L0_ffn_gate_up_w", "L0_ffn_down_w",
        "L0_ffn_shared_gate_w", "L0_ffn_shared_up_w", "L0_ffn_shared_down_w"]


def kernel(**inputs):
    import numpy as np
    import concourse.bacc as bacc
    from concourse.bass_utils import run_bass_kernel_spmd

    nc = bacc.Bacc("TRN2", target_bir_lowering=False, num_devices=1)
    arrays, args = {}, []
    for name in _INS:
        a = np.ascontiguousarray(inputs[name])
        arrays[f"in_{name}"] = a
        args.append(nc.dram_tensor(f"in_{name}", a.shape, mybir.dt.from_np(a.dtype), kind="ExternalInput").ap())
    shape = inputs["x"].shape
    args.append(nc.dram_tensor("out_0", shape, F32, kind="ExternalOutput").ap())
    build(nc, *args)
    r = run_bass_kernel_spmd(nc, [arrays], core_ids=[0])
    return r.results[0]["out_0"]
```

```python
from contextlib import ExitStack

import numpy as np

import concourse.bass as bass
from concourse import mybir

ALU = mybir.AluOpType
ACT = mybir.ActivationFunctionType
AX = mybir.AxisListType
F32 = mybir.dt.float32
F32R = mybir.dt.float32r
I32 = mybir.dt.int32

P = 128
BANK = 512
DK = 32
NEG = -1e30
LOWEST = -3.0e38

FIRST, MIDDLE, LAST = range(3)
MISC = [("k1_0", 0, 0), ("q1_0", 1, 1), ("k1_1", 2, 0), ("max0_1", 3, 1), ("q1_1", 4, 0), ("prev_ctx1_1", 4, 1),
        ("next_q0", 5, 0), ("prev_normed1", 6, 1), ("prev_hid0", 7, 0), ("prev_hid1", 8, 1), ("k1_2", 9, 0),
        ("q1_2", 10, 1), ("prev_hidT0", 10, 0), ("max1_0", 11, 1), ("k1_3", 12, 0), ("ctx0_0", 12, 1),
        ("q1_3", 13, 0), ("prev_hidT1", 14, 1),
        ("k0_0", 16, 0), ("q0_0", 17, 1), ("k0_1", 18, 0), ("max1_1", 19, 1), ("q0_1", 20, 0), ("ctx0_1", 20, 1),
        ("prev_router", 22, 0), ("normed0", 22, 1), ("next_q1", 23, 0), ("k0_2", 25, 1), ("q0_2", 26, 0),
        ("next_max0_0", 27, 1), ("k0_3", 28, 0), ("ctx1_0", 28, 1), ("q0_3", 29, 0)]
MISC_SETUP = [("wqT", 0), ("woT", 1), ("maskT", 0), ("q0", 0)] \
    + [(f"s0{c}_{h}", i) for h in range(4) for i, c in enumerate("kq")] + [("q1", 0), ("max0", 1)]
MISC_TAIL = [("tail_ctx1", 0), ("tail_normed", 1), ("tail_hid0", 0), ("tail_hid1", 1), ("tail_hidT0", 0),
             ("tail_hidT1", 1), ("tail_router", 0)]
BANK_OF = dict([(m[0], m[-1]) for m in MISC + MISC_SETUP + MISC_TAIL])


def misc_list(kind):
    return [m for m in MISC
            if not (kind == FIRST and m[0].startswith("prev"))
            and not (kind == LAST and (m[0].startswith("next") or m[0][:2] in ("k0", "q0")))]


def in_bank(uses, name):
    return [m[0] for m in uses if m[-1] == BANK_OF[name]]


def misc_count(b, kind, name):
    before = len(in_bank(MISC_SETUP, name))
    if kind != FIRST:
        before = before + len(in_bank(misc_list(FIRST), name)) + len(in_bank(misc_list(MIDDLE), name)) * (b - 1)
    return before + in_bank(misc_list(kind), name).index(name)


def setup_count(name):
    return in_bank(MISC_SETUP, name).index(name)


def tail_count(rows, name):
    return len(in_bank(MISC_SETUP, name)) + len(in_bank(misc_list(FIRST), name)) + len(in_bank(misc_list(LAST), name)) \
        + len(in_bank(misc_list(MIDDLE), name)) * (rows - 2) + in_bank(MISC_TAIL, name).index(name)


def fp32r(value):
    return float((np.float32(value).view(np.uint32) & np.uint32(0xFFFFF000)).view(np.float32))


def build(nc, x, cond, wq, wo, router_w, gate_up_w, down_w, sh_gate_w, sh_up_w, sh_down_w, out):
    B, D, T = x.shape
    E, _, F2 = gate_up_w.shape
    I = F2 // 2
    KD = D // P
    KT = T // P
    NQ = T // P
    G = D // P
    TOKENS = B * D
    TT = TOKENS // P
    SCALE = float(DK) ** -0.5
    assert T == BANK and KD == G == 2

    ctx = ExitStack()
    with ctx:
        def sb(name, shape, dt=F32):
            return ctx.enter_context(nc.sbuf_tensor(name, shape, dt))

        def sem(name):
            return ctx.enter_context(nc.semaphore(name))

        bank = [ctx.enter_context(nc.psum_tensor(f"bank{i}", [P, BANK], F32)) for i in range(8)]
        hidden = nc.dram_tensor("hidden_dram", [TOKENS, T], F32)

        ident = sb("ident", [P, P])
        logits_all = sb("logits_all", [P, TT, E])
        shared_in = [sb(f"shared_in{i}", [P, KT, I]) for i in range(2)]
        shared_out = sb("shared_out", [P, I // P, T])
        shared_loaded = sem("shared_loaded")

        attention = ExitStack()
        ctx.enter_context(attention)

        def sb(name, shape, dt=F32):
            return attention.enter_context(nc.sbuf_tensor(name, shape, dt))

        HPU = 4
        NJ = HPU * NQ
        BIAS_ROWS = 5
        MASK_ONE = 2.0 ** 50
        MASK_NEG = fp32r(NEG / SCALE / BIAS_ROWS / MASK_ONE)
        R_MASK, R_MAX = 3 * DK, 3 * DK + BIAS_ROWS
        K_MAX, K_ALL = R_MAX, R_MAX + 2

        logit_bank, key_bank, ctx_bank, misc = bank[0:2], bank[2:4], bank[4:6], bank[6:8]
        w_nat = sb("w_nat", [P, 2, KD, D])
        wqT = sb("wqT", [P, KD, D])
        woT = sb("woT", [P, KD, D])
        router_sb = sb("router_sb", [P, KT, E])
        x_row = sb("x_row", [P, KD, T])
        ident_r = sb("ident_r", [P, P], F32R)
        mask_nat = sb("mask_nat", [B * NQ, P])
        mask_cols = sb("mask_cols", [P, B * NQ])
        mask_now = sb("mask_now", [P, NQ])
        q_nat = sb("q_nat", [P, NQ, P])
        qm = sb("qm", [P, NQ, P])
        q_cols = [sb(f"q_cols{g}", [P, NQ, HPU, P], F32R) for g in range(G)]
        k_cols = [sb(f"k_cols{g}", [P, NQ, HPU, P], F32R) for g in range(G)]
        q_stack = [sb(f"q_stack{g}", [P, HPU, T], F32R) for g in range(G)]
        k_stack = [sb(f"k_stack{g}", [P, HPU, T], F32R) for g in range(G)]
        vals = [sb(f"vals{g}", [P, NQ, HPU, 2 * DK]) for g in range(G)]
        row_max = [sb(f"row_max{g}", [P, NJ]) for g in range(G)]
        max_hi = sb("max_hi", [2 * NQ, P], F32R)
        max_lo = sb("max_lo", [2 * NQ, P], F32R)
        probsT = [sb(f"probsT{i}", [P, T]) for i in range(4)]
        ctx_raw = [sb(f"ctx_raw{i}", [P, T]) for i in range(2)]
        inv_sum = [sb(f"inv_sum{i}", [P, NQ, 2]) for i in range(2)]
        ctx_nat = sb("ctx_nat", [P, NQ, HPU, DK])
        ctxn = sb("ctxn", [P, G, T])
        hid = sb("hid", [P, KD, T])
        hidT = sb("hidT", [P, KD, KT, P])

        x_loaded = sem("x_loaded")
        weights_loaded = [sem(f"weights_loaded{i}") for i in range(2)]
        router_loaded = sem("router_loaded")
        mask_loaded = sem("mask_loaded")
        max_loaded = [sem(f"max_loaded{g}") for g in range(G)]
        ident_cleared = sem("ident_cleared")
        ident_ready = sem("ident_ready")
        ident_r_ready = sem("ident_r_ready")
        ones_ready = sem("ones_ready")
        written = [sem(f"misc_written{i}") for i in range(2)]
        emptied = [sem(f"misc_emptied{i}") for i in range(2)]
        vals_ready = sem("vals_ready")
        cols_cleared = sem("cols_cleared")
        mask_copied = sem("mask_copied")
        cols_ready = sem("cols_ready")
        qm_ready = sem("qm_ready")
        hi_ready = sem("hi_ready")
        logits_written = sem("logits_written")
        logits_reduced = sem("logits_reduced")
        max_hi_ready = sem("max_hi_ready")
        keys_written = sem("keys_written")
        probs_ready = sem("probs_ready")
        weighed = sem("weighed")
        ctx_copied = sem("ctx_copied")
        inv_ready = sem("inv_ready")
        hidden_stored = sem("hidden_stored")
        pool_waits_passed = sem("pool_waits_passed")
        sp_waits_passed = sem("sp_waits_passed")

        block = attention.enter_context(nc.Block())

        def rows(eng, body):
            body(0, FIRST)
            with eng.Fori(1, B - 1) as b:
                body(b, MIDDLE)
            body(B - 1, LAST)

        def is_int(n, m):
            return isinstance(n, int) and n == m

        def tail(name):
            return tail_count(B, name)

        def four(m):
            return m[:, :].rearrange("p (k c) -> p k c", c=P)

        def logits_at(j):
            n = j + NJ - 3
            return (n // NJ, (n % NJ) // (2 * NQ), n % (2 * NQ))

        @block.sync
        def _(sp):
            def load_max(b, g, two, name, count):
                i = BANK_OF[name]
                sp.wait_ge(emptied[i], count + 1)
                for i, part in enumerate((max_hi, max_lo)):
                    dst = q_stack[g][R_MAX + i:R_MAX + i + 1, 2 * two:2 * two + 2, :]
                    sp.dma_start(dst.bitcast(F32).rearrange("o h (q p) -> o (h q) p", p=P), part[:, :].bitcast(F32))\
                        .then_inc(max_loaded[g], 16)

            def store_hidden(b, copied):
                for i in range(2):
                    sp.wait_ge(emptied[i], copied[i])
                    sp.sem_inc(sp_waits_passed, 1)
                sp.dma_start(hidden[bass.ds(b * D, D), :].rearrange("(k p) t -> p k t", p=P), hid[:, :, :])\
                    .then_inc(hidden_stored, 16)

            sp.sem_inc(hidden_stored, 16)
            sp.dma_start(w_nat[:, 0, :, :], wq.rearrange("(m p) d -> p m d", p=P)).then_inc(weights_loaded[0], 16)
            sp.dma_start(x_row[:, :, :], x[0].rearrange("(k p) t -> p k t", p=P)).then_inc(x_loaded, 16)
            sp.dma_start(mask_nat[:, :], cond.rearrange("b (q p) -> (b q) p", p=P)).then_inc(mask_loaded, 16)
            sp.dma_start(w_nat[:, 1, :, :], wo.rearrange("(m p) d -> p m d", p=P)).then_inc(weights_loaded[1], 16)
            sp.dma_start(router_sb[:, :, :], router_w.rearrange("(k p) e -> p k e", p=P)).then_inc(router_loaded, 16)
            load_max(0, 0, 0, "max0", setup_count("max0"))
            for dst, src in zip(shared_in, (sh_gate_w, sh_up_w)):
                sp.dma_start(dst[:, :, :], src.rearrange("(k p) i -> p k i", p=P)).then_inc(shared_loaded, 16)
            sp.dma_start(shared_out[:, :, :], sh_down_w.rearrange("(k p) d -> p k d", p=P)).then_inc(shared_loaded, 16)

            def body(b, kind):
                if kind != LAST:
                    sp.wait_ge(qm_ready, 2 * b + 2)
                    sp.sem_inc(sp_waits_passed, 1)
                    sp.dma_start(x_row[:, :, :], x[bass.ds(b + 1, 1)].rearrange("o (k p) t -> p (o k) t", p=P))\
                        .then_inc(x_loaded, 16)
                load_max(b, 0, 1, "max0_1", misc_count(b, kind, "max0_1"))
                if kind != FIRST:
                    store_hidden(b - 1, [misc_count(b, kind, f"prev_hid{i}") + 1 for i in range(2)])
                load_max(b, 1, 0, "max1_0", misc_count(b, kind, "max1_0"))
                load_max(b, 1, 1, "max1_1", misc_count(b, kind, "max1_1"))
                if kind != LAST:
                    load_max(b + 1, 0, 0, "next_max0_0", misc_count(b, kind, "next_max0_0"))

            rows(sp, body)
            store_hidden(B - 1, [tail(f"tail_hid{i}") + 1 for i in range(2)])
            sp.wait_ge(hidden_stored, 16 * B + 16)

        @block.gpsimd
        def _(pool):
            nc.gpsimd.memset(ident[:, :], 0.0).then_inc(ident_cleared, 1)
            pool.wait_ge(ident_cleared, 1)
            nc.gpsimd.affine_select(out=ident[:, :], in_=ident[:, :], compare_op=ALU.not_equal, fill=1.0,
                                    base=0, pattern=[[-1, P]], channel_multiplier=1).then_inc(ident_ready, 1)

            def split(b, g, name, copied):
                u = 2 * b + g
                if not is_int(u, 0):
                    pool.wait_ge(cols_ready, 4 * u)
                    pool.wait_ge(hi_ready, 4 * u)
                    pool.sem_inc(pool_waits_passed, 1)
                nc.gpsimd.tensor_copy(mask_now[:, :], mask_cols[:, bass.ds(b * NQ, NQ)]).then_inc(mask_copied, 1)
                pool.wait_ge(mask_copied, u + 1)
                pool.wait_ge(emptied[BANK_OF[name]], copied)
                nc.gpsimd.tensor_tensor(qm[:, :, :], q_nat[:, :, :],
                                        mask_now[:, :].unsqueeze(2).broadcast_to([P, NQ, P]), ALU.mult)\
                    .then_inc(qm_ready, 1)
                m = mask_now[:, :].unsqueeze(2).unsqueeze(3).broadcast_to([P, NQ, HPU, BIAS_ROWS])
                nc.gpsimd.tensor_scalar(q_cols[g][:, :, :, R_MASK:R_MAX], m, MASK_ONE, None, ALU.mult)\
                    .then_inc(cols_ready, 1)
                nc.gpsimd.tensor_scalar(k_cols[g][:, :, :, R_MASK:R_MAX], m, -MASK_NEG, MASK_NEG, ALU.mult, ALU.add)\
                    .then_inc(cols_ready, 1)
                pool.wait_ge(hi_ready, 4 * u + 1)
                whole = qm[:, :, :].rearrange("p k (h d) -> p k h d", h=HPU)
                for cols, at in ((q_cols[g], DK), (k_cols[g], 2 * DK)):
                    nc.gpsimd.tensor_tensor(cols[:, :, :, at:at + DK], whole,
                                            q_cols[g][:, :, :, 0:DK].bitcast(F32), ALU.subtract)\
                        .then_inc(cols_ready, 1)

            def values(u, g, steps_before):
                if steps_before is not None:
                    pool.wait_ge(weighed, steps_before)
                    pool.sem_inc(pool_waits_passed, 1)
                nc.gpsimd.tensor_copy(vals[g][:, :, :, 0:DK], q_nat[:, :, :].rearrange("p k (h d) -> p k h d", h=HPU))\
                    .then_inc(vals_ready, 1)

            pool.wait_ge(cols_cleared, 4)
            pool.wait_ge(emptied[BANK_OF["maskT"]], setup_count("maskT") + 1)
            split(0, 0, "q0", setup_count("q0") + 1)
            values(0, 0, None)
            split(0, 1, "q1", setup_count("q1") + 1)

            def body(b, kind):
                values(2 * b + 1, 1, None if kind == FIRST else 2 * NJ * b)
                if kind != LAST:
                    split(b + 1, 0, "next_q0", misc_count(b, kind, "next_q0") + 1)
                    values(2 * b + 2, 0, 2 * NJ * b + NJ)
                    split(b + 1, 1, "next_q1", misc_count(b, kind, "next_q1") + 1)

            rows(pool, body)

        @block.tensor
        def _(pe):
            def turn(dst, src, n=P):
                return nc.tensor.transpose(dst, src, ident[0:n, 0:n])

            def turn_blocks(dst, src, n):
                for k in range(n):
                    last = turn(dst[:, k * P:(k + 1) * P], src(k))
                return last

            def project_q(m, b, g):
                pe.wait_ge(x_loaded, 16 * (b + 1))
                for q in range(NQ):
                    for k in range(KD):
                        last = nc.tensor.matmul(m[:, q * P:(q + 1) * P], x_row[:, k, q * P:(q + 1) * P],
                                                wqT[:, k, g * P:(g + 1) * P], start=(k == 0), stop=(k == KD - 1))
                return last

            def turn_cols(m, u, cols, h):
                pe.wait_ge(hi_ready, 4 * u + 4)
                pe.wait_ge(cols_ready, 4 * u + 4)
                for k in range(NQ):
                    last = nc.tensor.matmul(m[:, k * P:(k + 1) * P], cols[:, k, h, :], ident_r[:, :],
                                            start=True, stop=True)
                return last

            def turn_max(m, u, g, two):
                pe.wait_ge(logits_reduced, 4 * NQ * u + 2 * NQ * (two + 1))
                return turn(m[0:2 * NQ, 0:P], row_max[g][:, 2 * NQ * two:2 * NQ * (two + 1)])

            def turn_ctx(m, u, two):
                pe.wait_ge(ctx_copied, 2 * u + two + 1)
                return turn_blocks(m, lambda k: ctx_raw[two][:, k * P:(k + 1) * P], NQ)

            def turn_normed(m, name, count):
                pe.wait_ge(emptied[BANK_OF[name]], count)
                return turn_blocks(m, lambda k: ctx_nat[:, k, :, :].rearrange("p h d -> p (h d)"), NQ)

            def hidden_half(m, e, copied):
                pe.wait_ge(emptied[BANK_OF["prev_normed1"]], copied)
                for g in range(G):
                    last = nc.tensor.matmul(m[:, :], woT[:, g, e * P:(e + 1) * P], ctxn[:, g, :],
                                            start=(g == 0), stop=(g == G - 1))
                return last

            def turn_hidden(m, e, copied):
                pe.wait_ge(emptied[BANK_OF[f"prev_hid{e}"]], copied)
                return turn_blocks(m, lambda k: hid[:, e, k * P:(k + 1) * P], KT)

            def route(m, copied):
                for e in range(KD):
                    pe.wait_ge(emptied[BANK_OF[f"prev_hidT{e}"]], copied[e])
                    for k in range(KT):
                        last = nc.tensor.matmul(m[:, e * E:(e + 1) * E], hidT[:, e, k, :], router_sb[:, k, :],
                                                start=(k == 0), stop=(k == KT - 1))
                return last

            def use(name, count, f, *args):
                i = BANK_OF[name]
                if not is_int(count, 0):
                    pe.wait_ge(emptied[i], count)
                f(misc[i], *args).then_inc(written[i], 1)

            def use_misc(b, kind, slot):
                for name, s, _ in misc_list(kind):
                    if s != slot:
                        continue
                    c = misc_count(b, kind, name)
                    u = 2 * b
                    done = lambda n: misc_count(b, kind, n) + 1
                    job = {
                        "prev_ctx1_1": (turn_ctx, u - 1, 1), "ctx0_0": (turn_ctx, u, 0),
                        "ctx0_1": (turn_ctx, u, 1), "ctx1_0": (turn_ctx, u + 1, 0),
                        "max0_1": (turn_max, u, 0, 1), "max1_0": (turn_max, u + 1, 1, 0),
                        "max1_1": (turn_max, u + 1, 1, 1), "next_max0_0": (turn_max, u + 2, 0, 0),
                        "prev_normed1": (turn_normed, "prev_ctx1_1", "prev_ctx1_1"),
                        "normed0": (turn_normed, "ctx0_1", "ctx0_1"),
                        "next_q0": (project_q, b + 1, 0), "next_q1": (project_q, b + 1, 1)}
                    if name[1] in "01" and name[0] in "qk":
                        h, g = int(name[-1]), int(name[1])
                        j = (turn_cols, u + 1 if g else u + 2, (q_cols if name[0] == "q" else k_cols)[g], h)
                    elif name.startswith("prev_hid") or name == "prev_router":
                        if name == "prev_router":
                            j = (route, [done("prev_hidT0"), done("prev_hidT1")])
                        elif "T" in name:
                            j = (turn_hidden, int(name[-1]), done(f"prev_hid{name[-1]}"))
                        else:
                            j = (hidden_half, int(name[-1]), done("prev_normed1"))
                    else:
                        j = job[name]
                        if j[0] is turn_normed:
                            j = (turn_normed, j[1], done(j[2]))
                    use(name, c, *j)

            def find_logits(u, g, two, i):
                n = 4 * NQ * u + 2 * NQ * two + i
                h, q = 2 * two + i // NQ, i % NQ
                if not (isinstance(n, int) and n < 2):
                    pe.wait_ge(logits_reduced, n - 1)
                nc.tensor.matmul(logit_bank[i % 2][:, :], q_stack[g][0:K_MAX, h, q * P:(q + 1) * P],
                                 k_stack[g][0:K_MAX, h, :], start=True, stop=True).then_inc(logits_written, 1)

            def stack_ready(name, count):
                pe.wait_ge(emptied[BANK_OF[name]], count + 1)

            def head_and_block(j):
                two, k, h = j // (2 * NQ), (j // 2) % NQ, j % 2
                return two, k, 2 * two + h, h

            def find_keys(b, g, j):
                n = NJ * (2 * b + g) + j
                two, k, h, _ = head_and_block(j)
                if j == 2:
                    pe.wait_ge(vals_ready, 2 * b + g + 1)
                if j % (2 * NQ) == 0:
                    pe.wait_ge(max_loaded[g], 64 * b + 32 * (two + 1))
                if not (isinstance(n, int) and n < 2):
                    pe.wait_ge(probs_ready, n - 1)
                nc.tensor.matmul(key_bank[j % 2][:, :], k_stack[g][0:K_ALL, h, k * P:(k + 1) * P],
                                 q_stack[g][0:K_ALL, h, :], start=True, stop=True).then_inc(keys_written, 1)

            def weigh(u, g, j):
                n = NJ * u + j
                two, k, h, half = head_and_block(j)
                pe.wait_ge(probs_ready, n + 1)
                if k == 0 and half == 0:
                    if not (isinstance(u, int) and 2 * u + two < 2):
                        pe.wait_ge(ctx_copied, 2 * u + two - 1)
                nc.tensor.matmul(ctx_bank[two][half * 64:half * 64 + 64, :], vals[g][:, k, h, :],
                                 probsT[j % 4][:, :], start=(k == 0), stop=(k == NQ - 1)).then_inc(weighed, 1)

            pe.wait_ge(ident_ready, 1)
            for i, name in enumerate(("wqT", "woT")):
                pe.wait_ge(weights_loaded[i], 16)
                last = None
                for k in range(KD):
                    for m in range(KD):
                        c = k * D + m * P
                        last = turn(misc[BANK_OF[name]][:, c:c + P], w_nat[:, i, m, k * P:(k + 1) * P])
                last.then_inc(written[BANK_OF[name]], 1)
            pe.wait_ge(mask_loaded, 16)
            use("maskT", setup_count("maskT"), lambda m: turn(m[:, 0:B * NQ], mask_nat[:, :], B * NQ))
            pe.wait_ge(emptied[BANK_OF["wqT"]], 1)
            use("q0", setup_count("q0"), project_q, 0, 0)
            pe.wait_ge(ident_r_ready, 1)
            for name, _ in MISC_SETUP:
                if name.startswith("s0"):
                    use(name, setup_count(name), turn_cols, 0, (q_cols if name[2] == "q" else k_cols)[0], int(name[-1]))
                if name == "q1":
                    use(name, setup_count(name), project_q, 0, 1)
            for name, _ in MISC_SETUP:
                if name.startswith("s0"):
                    stack_ready(name, setup_count(name))
            for i in range(2 * NQ):
                find_logits(0, 0, 0, i)
            use("max0", setup_count("max0"), turn_max, 0, 0, 0)
            for i in range(5):
                find_logits(0, 0, 1, i)
            pe.wait_ge(router_loaded, 16)
            pe.wait_ge(ones_ready, G)
            pe.wait_ge(emptied[BANK_OF["woT"]], setup_count("woT") + 1)

            def body(b, kind):
                for s in range(2 * NJ):
                    g, j = divmod(s, NJ)
                    u = 2 * b + g
                    last_unit = kind == LAST and g == 1
                    du, two, i = logits_at(j)
                    if not (last_unit and du):
                        if i % NQ == 0:
                            stacks = [f"{c}{1 - g}_{2 * two + i // NQ}" for c in "kq"]
                            for name in {BANK_OF[m]: m for m in stacks}.values():
                                stack_ready(name, misc_count(b, kind, name))
                        find_logits(u + du, g ^ du, two, i)
                    find_keys(b, g, j)
                    use_misc(b, kind, s)
                    if kind != FIRST or s >= 2:
                        if j >= 2:
                            weigh(u, g, j - 2)
                        else:
                            weigh(u - 1, 1 - g, j - 2 + NJ)

            rows(pe, body)
            u = 2 * B - 1
            for j in (NJ - 2, NJ - 1):
                weigh(u, 1, j)
            use("tail_ctx1", tail("tail_ctx1"), turn_ctx, u, 1)
            use("tail_normed", tail("tail_normed"), turn_normed, "tail_ctx1", tail("tail_ctx1") + 1)
            for e in range(2):
                use(f"tail_hid{e}", tail(f"tail_hid{e}"), hidden_half, e, tail("tail_normed") + 1)
            for e in range(2):
                use(f"tail_hidT{e}", tail(f"tail_hidT{e}"), turn_hidden, e, tail(f"tail_hid{e}") + 1)
            use("tail_router", tail("tail_router"), route, [tail(f"tail_hidT{e}") + 1 for e in range(2)])

        @block.scalar
        def _(act):
            def empty(name, count, dst, view=lambda m: m[:, :]):
                i = BANK_OF[name]
                act.wait_ge(written[i], count + 1)
                nc.scalar.activation(dst, view(misc[i]), ACT.Copy).then_inc(emptied[i], 1)

            def empty_q(name, count, u):
                if not is_int(u, 0):
                    act.wait_ge(qm_ready, u)
                    act.wait_ge(vals_ready, u)
                empty(name, count, q_nat[:, :, :], four)

            def upper(u, g, parts):
                act.wait_ge(qm_ready, u + 1)
                whole = qm[:, :, :].rearrange("p k (h d) -> p k h d", h=HPU)
                places = (q_cols[g], 0), (q_cols[g], 2 * DK), (k_cols[g], 0), (k_cols[g], DK)
                for cols, at in places[parts]:
                    nc.scalar.activation(cols[:, :, :, at:at + DK], whole, ACT.Copy)\
                        .then_inc(hi_ready, 1)

            def empty_stack(name, count, stack, h):
                empty(name, count, stack[:, h, :])

            def upper_max(name, count, n):
                i = BANK_OF[name]
                act.wait_ge(written[i], count + 1)
                if not is_int(n, 0):
                    u2, g, two = max_place(n)
                    act.wait_ge(max_loaded[g], u2)
                nc.scalar.activation(max_hi[:, :], misc[i][0:2 * NQ, 0:P], ACT.Copy, scale=-1.0).then_inc(max_hi_ready, 1)

            def max_place(n):
                b, g, two = n
                return 64 * b + 32 * (two + 1), g, two

            def exp(n, j):
                act.wait_ge(keys_written, n + 1)
                if not (isinstance(n, int) and n < 4):
                    act.wait_ge(weighed, n - 3)
                nc.scalar.activation(probsT[j % 4][:, :], key_bank[j % 2][:, :], ACT.Exp, scale=SCALE)\
                    .then_inc(probs_ready, 1)

            def copy_ctx(u, two):
                act.wait_ge(weighed, NJ * u + 2 * NQ * (two + 1))
                nc.scalar.activation(ctx_raw[two][:, :], ctx_bank[two][:, :], ACT.Copy).then_inc(ctx_copied, 1)

            def empty_misc(b, kind, slot):
                for name, s, _ in misc_list(kind):
                    if s != slot:
                        continue
                    c = misc_count(b, kind, name)
                    if name in ("next_q0", "next_q1"):
                        empty_q(name, c, 2 * b + 2 + int(name[-1]))
                    elif name[0] == "k":
                        empty_stack(name, c, k_stack[int(name[1])], int(name[-1]))
                    elif name == "prev_normed1":
                        empty(name, c, ctxn[:, 1, :])
                    elif name == "normed0":
                        empty(name, c, ctxn[:, 0, :])
                    elif name == "prev_hid0":
                        act.wait_ge(hidden_stored, 16 * b)
                        empty(name, c, hid[:, 0, :])
                    elif name == "prev_hidT0":
                        empty(name, c, hidT[:, 0, :, :], four)
                    elif name == "max0_1":
                        upper_max(name, c, (b, 0, 0))
                    elif name == "max1_0":
                        upper_max(name, c, (b, 0, 1))
                    elif name == "max1_1":
                        upper_max(name, c, (b, 1, 0))
                    elif name == "next_max0_0":
                        upper_max(name, c, (b, 1, 1))

            empty("wqT", 0, wqT[:, :, :], lambda m: m[:, :].rearrange("p (k c) -> p k c", k=KD))
            empty("woT", 0, woT[:, :, :], lambda m: m[:, :].rearrange("p (k c) -> p k c", k=KD))
            nc.scalar.activation(ident_r[:, :], ident[:, :], ACT.Copy).then_inc(ident_r_ready, 1)
            empty("maskT", setup_count("maskT"), mask_cols[:, :], lambda m: m[:, 0:B * NQ])
            empty_q("q0", setup_count("q0"), 0)
            upper(0, 0, slice(0, 4))
            for name, _ in MISC_SETUP:
                if name.startswith("s0k"):
                    empty_stack(name, setup_count(name), k_stack[0], int(name[-1]))
            empty_q("q1", setup_count("q1"), 1)
            upper(1, 1, slice(0, 4))
            upper_max("max0", setup_count("max0"), 0)

            def body(b, kind):
                for s in range(2 * NJ):
                    g, j = divmod(s, NJ)
                    exp(NJ * (2 * b + g) + j, j)
                    if j == 1 and (kind != FIRST or g == 1):
                        copy_ctx(2 * b + g - 1, 1)
                    if j == 2 * NQ + 1:
                        copy_ctx(2 * b + g, 0)
                    empty_misc(b, kind, s)
                    if 7 <= j < 11 and kind != LAST:
                        upper(2 * b + 2 + g, g, slice(j - 7, j - 6))

            rows(act, body)
            copy_ctx(2 * B - 1, 1)
            empty("tail_normed", tail("tail_normed"), ctxn[:, 1, :])
            act.wait_ge(hidden_stored, 16 * B)
            empty("tail_hid0", tail("tail_hid0"), hid[:, 0, :])
            empty("tail_hidT0", tail("tail_hidT0"), hidT[:, 0, :, :], four)

        @block.vector
        def _(dve):
            def empty(name, count, dst, view=lambda m: m[:, :]):
                i = BANK_OF[name]
                dve.wait_ge(written[i], count + 1)
                nc.vector.tensor_copy(dst, view(misc[i])).then_inc(emptied[i], 1)

            def reduce(u, g, two, i):
                dve.wait_ge(logits_written, 4 * NQ * u + 2 * NQ * two + i + 1)
                c = 2 * NQ * two + i
                nc.vector.tensor_reduce(row_max[g][:, c:c + 1], logit_bank[i % 2][:, :], AX.X, ALU.max)\
                    .then_inc(logits_reduced, 1)

            def lower_max(name, count, n):
                i = BANK_OF[name]
                dve.wait_ge(max_hi_ready, n + 1)
                nc.vector.scalar_tensor_tensor(out=max_lo[:, :], in0=misc[i][0:2 * NQ, 0:P], scalar=-1.0,
                                               in1=max_hi[:, :].bitcast(F32), op0=ALU.mult, op1=ALU.subtract)\
                    .then_inc(emptied[i], 1)

            def normalise(name, count, u, two):
                i = BANK_OF[name]
                n = 2 * u + two
                v = misc[i][:, :].rearrange("p (k h c) -> p k h c", k=NQ, h=2)
                dve.wait_ge(written[i], count + 1)
                nc.vector.reciprocal(inv_sum[two][:, :, :], v[:, :, :, DK]).then_inc(inv_ready, 1)
                dve.wait_ge(inv_ready, n + 1)
                nc.vector.tensor_tensor(ctx_nat[:, :, 2 * two:2 * two + 2, :], v[:, :, :, 0:DK],
                                        inv_sum[two][:, :, :].unsqueeze(3).broadcast_to([P, NQ, 2, DK]), ALU.mult)\
                    .then_inc(emptied[i], 1)

            def empty_misc(b, kind, slot):
                for name, s, _ in misc_list(kind):
                    if s != slot:
                        continue
                    c = misc_count(b, kind, name)
                    if name[0] == "q":
                        empty(name, c, q_stack[int(name[1])][:, int(name[-1]), :])
                    elif name == "prev_hid1":
                        dve.wait_ge(hidden_stored, 16 * b)
                        empty(name, c, hid[:, 1, :])
                    elif name == "prev_hidT1":
                        empty(name, c, hidT[:, 1, :, :], four)
                    elif name == "prev_router":
                        empty(name, c, logits_all[:, bass.ds((b - 1) * KD, KD), :],
                              lambda m: m[:, 0:KD * E].rearrange("p (k e) -> p k e", k=KD))
                    elif name == "max0_1":
                        lower_max(name, c, 4 * b + 1)
                    elif name == "max1_0":
                        lower_max(name, c, 4 * b + 2)
                    elif name == "max1_1":
                        lower_max(name, c, 4 * b + 3)
                    elif name == "next_max0_0":
                        lower_max(name, c, 4 * b + 4)
                    elif name == "prev_ctx1_1":
                        normalise(name, c, 2 * b - 1, 1)
                    elif name == "ctx0_0":
                        normalise(name, c, 2 * b, 0)
                    elif name == "ctx0_1":
                        normalise(name, c, 2 * b, 1)
                    elif name == "ctx1_0":
                        normalise(name, c, 2 * b + 1, 0)

            for g in range(G):
                nc.vector.memset(k_cols[g][:, :, :, R_MAX:P].bitcast(F32), 1.0).then_inc(cols_cleared, 1)
                nc.vector.memset(q_cols[g][:, :, :, R_MAX:P].bitcast(F32), 0.0).then_inc(cols_cleared, 1)
                nc.vector.memset(vals[g][:, :, :, DK:2 * DK], 1.0).then_inc(ones_ready, 1)
            for name, _ in MISC_SETUP:
                if name.startswith("s0q"):
                    empty(name, setup_count(name), q_stack[0][:, int(name[-1]), :])
            for i in range(2 * NQ):
                reduce(0, 0, 0, i)
            lower_max("max0", setup_count("max0"), 0)
            for i in range(5):
                reduce(0, 0, 1, i)

            def body(b, kind):
                for s in range(2 * NJ):
                    g, j = divmod(s, NJ)
                    u = 2 * b + g
                    du, two, i = logits_at(j)
                    if not (kind == LAST and g == 1 and du):
                        reduce(u + du, g ^ du, two, i)
                    empty_misc(b, kind, s)

            rows(dve, body)
            normalise("tail_ctx1", tail("tail_ctx1"), 2 * B - 1, 1)
            dve.wait_ge(hidden_stored, 16 * B)
            empty("tail_hid1", tail("tail_hid1"), hid[:, 1, :])
            empty("tail_hidT1", tail("tail_hidT1"), hidT[:, 1, :, :], four)
            empty("tail_router", tail("tail_router"), logits_all[:, (B - 1) * KD:B * KD, :],
                  lambda m: m[:, 0:KD * E].rearrange("p (k e) -> p k e", k=KD))


        attention.close()

        NT = -(-(2 * TOKENS + E * (P - 1)) // (2 * P)) * 2
        KI = I // P

        def sb(name, shape, dt=F32):
            return ctx.enter_context(nc.sbuf_tensor(name, shape, dt))

        gate_up_sb = sb("gate_up_sb", [P, E * KT, F2])
        down_sb = sb("down_sb", [P, E * KI, T])
        experts_loaded = sem("experts_loaded")
        shared_in_hi, shared_in_lo = ([sb(f"shared_in_{part}{i}", [P, KT, I], F32R) for i in range(2)]
                                      for part in ("hi", "lo"))
        shared_out_hi, shared_out_lo = (sb(f"shared_out_{part}", [P, KI, T], F32R) for part in ("hi", "lo"))
        shared_parts = list(zip(shared_in_hi + [shared_out_hi], shared_in_lo + [shared_out_lo],
                                shared_in + [shared_out]))
        slot_token = sb("slot_token", [P, NT], I32)
        slot_prob = sb("slot_prob", [P, NT])
        tile_expert = sb("tile_expert", [1, NT], I32)
        token_slot = sb("token_slot", [P, 2, TT], I32)
        expert_rows = nc.dram_tensor("expert_rows_dram", [NT * P, T], F32)

        routing = ExitStack()
        ctx.enter_context(routing)
        with routing:
            def rb(name, shape, dt=F32):
                return routing.enter_context(nc.sbuf_tensor(name, shape, dt))

            GROUP = 8
            assert TT % GROUP == 0 and TOKENS <= 4096
            expert_no = rb("expert_no", [P, TT, E])
            before_e = rb("before_e", [P, E, E])
            tile_no = rb("tile_no", [P, NT])
            place_no = rb("place_no", [P, P])
            token_no = rb("token_no", [P, TT])
            place_i = rb("place_i", [P, P], I32)
            earlier = rb("earlier", [P, P])
            ones = rb("ones", [P, P])
            best = rb("best", [P, 2, TT])
            chosen = [rb(f"chosen{c}", [P, TT, E]) for c in range(2)]
            rest = rb("rest", [P, TT, E])
            cand = rb("cand", [P, TT, E])
            cand_min = rb("cand_min", [P, TT])
            both = rb("both", [P, TT, E])
            sigm = rb("sigm", [P, 2, TT])
            prob = rb("prob", [P, 2, TT])
            totals = rb("totals", [P, TT, E])
            cum = [rb(f"cum{i}", [P, TT, E]) for i in range(2)]
            slots = rb("slots", [P, TT, E])
            over = rb("over", [P, E, TT])
            tiles_of = rb("tiles_of", [P, E])
            pairs = rb("pairs", [P, E, E])
            first_tile = rb("first_tile", [P, E])
            end_tile = rb("end_tile", [P, E])
            passed = rb("passed", [P, NT, E - 1])
            expert_f = rb("expert_f", [P, NT])
            slot_f = rb("slot_f", [P, 2, TT])
            slot_i = rb("slot_i", [P, 2, TT], I32)
            s_tile_i = rb("s_tile_i", [P, 2, TT], I32)
            s_place_i = rb("s_place_i", [P, 2, TT], I32)
            s_tile = rb("s_tile", [P, 2, TT])
            s_place = rb("s_place", [P, 2, TT])
            prob_hi = rb("prob_hi", [P, 2, TT], F32R)
            prob_lo = rb("prob_lo", [P, 2, TT])
            prob_sum = rb("prob_sum", [P, NT])
            at_place = [rb(f"at_place{i}", [P, GROUP, P], F32R) for i in range(2)]
            tile_hot = [rb(f"tile_hot{i}", [P, GROUP, NT]) for i in range(2)]
            at_tile = [rb(f"at_tile{i}", [P, GROUP, 3, NT], F32R) for i in range(2)]

            def rsem(name):
                return routing.enter_context(nc.semaphore(name))

            constants_ready = rsem("constants_ready")
            shared_hi_ready = rsem("shared_hi_ready")
            chain = rsem("chain")
            best_ready = rsem("best_ready")
            sigm_ready = rsem("sigm_ready")
            both_ready = rsem("both_ready")
            counted = rsem("counted")
            tiles_marked = rsem("tiles_marked")
            pool_parts_ready = rsem("pool_parts_ready")
            tiles_ready = rsem("tiles_ready")
            group_added = rsem("group_added")
            block2 = routing.enter_context(nc.Block())

            @block2.sync
            def _(sp):
                for e in range(E):
                    sp.dma_start(gate_up_sb[:, e * KT:(e + 1) * KT, :],
                                 gate_up_w[e].rearrange("(k p) f -> p k f", p=P)).then_inc(experts_loaded, 16)
                    sp.dma_start(down_sb[:, e * KI:(e + 1) * KI, :],
                                 down_w[e].rearrange("(k p) d -> p k d", p=P)).then_inc(experts_loaded, 16)

            @block2.gpsimd
            def _(pool):
                kw = dict(allow_small_or_imprecise_dtypes=True)
                nc.gpsimd.iota(expert_no[:, :, :], [[0, TT], [1, E]], base=0, channel_multiplier=0, **kw)
                nc.gpsimd.iota(tile_no[:, :], [[1, NT]], base=0, channel_multiplier=0, **kw)
                nc.gpsimd.iota(place_no[:, :], [[1, P]], base=0, channel_multiplier=0, **kw)
                nc.gpsimd.iota(token_no[:, :], [[P, TT]], base=0, channel_multiplier=1, **kw)
                nc.gpsimd.memset(ones[:, :], 1.0).then_inc(constants_ready, 1)
                nc.gpsimd.memset(before_e[:, :, :], 1.0).then_inc(constants_ready, 1)
                pool.wait_ge(constants_ready, 2)
                nc.gpsimd.affine_select(out=earlier[:, :], in_=ones[:, :], compare_op=ALU.is_gt, fill=0.0,
                                        base=0, pattern=[[1, P]], channel_multiplier=-1)
                nc.gpsimd.affine_select(out=before_e[:, :, :], in_=before_e[:, :, :], compare_op=ALU.is_gt, fill=0.0,
                                        base=0, pattern=[[1, E], [-1, E]], channel_multiplier=0)\
                    .then_inc(constants_ready, 1)
                for n, (hi, lo, w) in enumerate(shared_parts):
                    pool.wait_ge(shared_hi_ready, n + 1)
                    nc.gpsimd.tensor_tensor(lo[:, :, :], w[:, :, :], hi[:, :, :].bitcast(F32), ALU.subtract)
                for q in range(2 * TT // GROUP):
                    c, t = divmod(q * GROUP, TT)
                    pool.wait_ge(tiles_marked, q + 1)
                    wide = [P, GROUP, NT]
                    for k, what in (0, token_no[:, t:t + GROUP]), (2, prob_lo[:, c, t:t + GROUP]):
                        last = nc.gpsimd.tensor_tensor(at_tile[q % 2][:, :, k, :], tile_hot[q % 2][:, :, :],
                                                       what.unsqueeze(2).broadcast_to(wide), ALU.mult)
                    last.then_inc(pool_parts_ready, 1)

            @block2.scalar
            def _(act):
                act.wait_ge(shared_loaded, 48)
                for hi, _, w in shared_parts:
                    nc.scalar.activation(hi[:, :, :], w[:, :, :], ACT.Copy).then_inc(shared_hi_ready, 1)
                act.wait_ge(best_ready, 1)
                nc.scalar.activation(sigm[:, :, :], best[:, :, :], ACT.Exp, scale=-1.0).then_inc(sigm_ready, 1)

            @block2.tensor
            def _(pe):
                pe.wait_ge(constants_ready, 3)
                pe.wait_ge(both_ready, 1)
                flat = both[:, :, :].rearrange("p t e -> p (t e)")
                nc.tensor.matmul(bank[0][:, 0:TT * E], earlier[:, :], flat, start=True, stop=True)
                nc.tensor.matmul(bank[1][:, 0:TT * E], ones[:, :], flat, start=True, stop=True).then_inc(counted, 1)
                for q in range(2 * TT // GROUP):
                    pe.wait_ge(tiles_ready, q + 1)
                    pe.wait_ge(pool_parts_ready, q + 1)
                    for k in range(GROUP):
                        n = q * GROUP + k
                        last = nc.tensor.matmul(bank[2][:, 0:3 * NT], at_place[q % 2][:, k, :],
                                                at_tile[q % 2][:, k, :, :].rearrange("p a b -> p (a b)"),
                                                start=(n == 0), stop=(n == 2 * TT - 1))
                    last.then_inc(group_added, 1)

            @block2.vector
            def _(dve):
                done = [0]

                def link(ins):
                    done[0] += 1
                    ins.then_inc(chain, 1)
                    dve.wait_ge(chain, done[0])

                v = nc.vector
                wide = [P, TT, E]
                dve.wait_ge(constants_ready, 3)
                src = logits_all
                for c in range(2):
                    link(v.tensor_reduce(best[:, c, :], src[:, :, :], AX.X, ALU.max))
                    link(v.tensor_tensor(cand[:, :, :], src[:, :, :], best[:, c, :].unsqueeze(2).broadcast_to(wide),
                                         ALU.is_equal))
                    link(v.scalar_tensor_tensor(out=cand[:, :, :], in0=cand[:, :, :], scalar=-float(E),
                                                in1=expert_no[:, :, :], op0=ALU.mult, op1=ALU.add))
                    link(v.tensor_reduce(cand_min[:, :], cand[:, :, :], AX.X, ALU.min))
                    link(v.tensor_tensor(chosen[c][:, :, :], cand[:, :, :],
                                         cand_min[:, :].unsqueeze(2).broadcast_to(wide), ALU.is_equal))
                    if c == 0:
                        link(v.scalar_tensor_tensor(out=rest[:, :, :], in0=chosen[0][:, :, :], scalar=LOWEST,
                                                    in1=logits_all[:, :, :], op0=ALU.mult, op1=ALU.add))
                        src = rest
                v.tensor_tensor(both[:, :, :], chosen[0][:, :, :], chosen[1][:, :, :], ALU.add).then_inc(both_ready, 1)
                v.tensor_copy(cand_min[:, :], best[:, 1, :]).then_inc(best_ready, 1)
                dve.wait_ge(sigm_ready, 1)
                link(v.tensor_scalar(sigm[:, :, :], sigm[:, :, :], 1.0, None, ALU.add))
                link(v.reciprocal(prob[:, :, :], sigm[:, :, :]))
                dve.wait_ge(counted, 1)
                link(v.tensor_copy(totals[:, :, :], bank[1][:, 0:TT * E].rearrange("p (t e) -> p t e", e=E)))
                src, step, i = totals, 1, 0
                while step < TT:
                    v.tensor_copy(cum[i][:, 0:step, :], src[:, 0:step, :])
                    link(v.tensor_tensor(cum[i][:, step:TT, :], src[:, step:TT, :], src[:, 0:TT - step, :], ALU.add))
                    src, step, i = cum[i], 2 * step, 1 - i
                inclusive, spare = src, cum[i]
                link(v.tensor_tensor(spare[:, :, :], inclusive[:, :, :], totals[:, :, :], ALU.subtract))
                link(v.tensor_tensor(slots[:, :, :], spare[:, :, :],
                                     bank[0][:, 0:TT * E].rearrange("p (t e) -> p t e", e=E), ALU.add))
                link(v.tensor_scalar(rest[:, 0, :], inclusive[:, TT - 1, :], 1.0 / P, None, ALU.mult))
                link(v.tensor_tensor(over[:, :, :], rest[:, 0, :].unsqueeze(2).broadcast_to([P, E, TT]),
                                     tile_no[:, 0:TT].unsqueeze(1).broadcast_to([P, E, TT]), ALU.is_gt))
                link(v.tensor_reduce(tiles_of[:, :], over[:, :, :], AX.X, ALU.add))
                link(v.tensor_tensor(pairs[:, :, :], before_e[:, :, :],
                                     tiles_of[:, :].unsqueeze(1).broadcast_to([P, E, E]), ALU.mult))
                link(v.tensor_reduce(first_tile[:, :], pairs[:, :, :], AX.X, ALU.add))
                link(v.tensor_tensor(end_tile[:, :], first_tile[:, :], tiles_of[:, :], ALU.add))
                link(v.tensor_tensor(passed[:, :, :], end_tile[:, 0:E - 1].unsqueeze(1).broadcast_to([P, NT, E - 1]),
                                     tile_no[:, :].unsqueeze(2).broadcast_to([P, NT, E - 1]), ALU.is_le))
                link(v.tensor_reduce(expert_f[:, :], passed[:, :, :], AX.X, ALU.add))
                v.tensor_copy(tile_expert[:, :], expert_f[0:1, :])
                link(v.scalar_tensor_tensor(out=slots[:, :, :],
                                            in0=first_tile[:, :].unsqueeze(1).broadcast_to(wide), scalar=float(P),
                                            in1=slots[:, :, :], op0=ALU.mult, op1=ALU.add))
                for c in range(2):
                    link(v.tensor_tensor(cand[:, :, :], chosen[c][:, :, :], slots[:, :, :], ALU.mult))
                    link(v.tensor_reduce(slot_f[:, c, :], cand[:, :, :], AX.X, ALU.add))
                v.tensor_copy(token_slot[:, :, :], slot_f[:, :, :])
                link(v.tensor_copy(slot_i[:, :, :], slot_f[:, :, :]))
                v.tensor_scalar(s_tile_i[:, :, :], slot_i[:, :, :], P.bit_length() - 1, None, ALU.logical_shift_right)
                link(v.tensor_scalar(s_place_i[:, :, :], slot_i[:, :, :], P - 1, None, ALU.bitwise_and))
                v.tensor_copy(s_tile[:, :, :], s_tile_i[:, :, :])
                v.tensor_copy(prob_hi[:, :, :], prob[:, :, :])
                link(v.tensor_copy(s_place[:, :, :], s_place_i[:, :, :]))
                link(v.tensor_tensor(prob_lo[:, :, :], prob[:, :, :], prob_hi[:, :, :].bitcast(F32), ALU.subtract))
                for q in range(2 * TT // GROUP):
                    c, t = divmod(q * GROUP, TT)
                    if q >= 2:
                        dve.wait_ge(group_added, q - 1)
                    wide, wide_p = [P, GROUP, NT], [P, GROUP, P]
                    v.tensor_tensor(tile_hot[q % 2][:, :, :], tile_no[:, :].unsqueeze(1).broadcast_to(wide),
                                    s_tile[:, c, t:t + GROUP].unsqueeze(2).broadcast_to(wide), ALU.is_equal)\
                        .then_inc(tiles_marked, 1)
                    v.tensor_tensor(at_place[q % 2][:, :, :], place_no[:, :].unsqueeze(1).broadcast_to(wide_p),
                                    s_place[:, c, t:t + GROUP].unsqueeze(2).broadcast_to(wide_p), ALU.is_equal)
                    dve.wait_ge(tiles_marked, q + 1)
                    hi = prob_hi[:, c, t:t + GROUP].bitcast(F32).unsqueeze(2).broadcast_to(wide)
                    v.tensor_tensor(at_tile[q % 2][:, :, 1, :], tile_hot[q % 2][:, :, :], hi, ALU.mult)\
                        .then_inc(tiles_ready, 1)
                dve.wait_ge(group_added, 2 * TT // GROUP)
                v.tensor_copy(slot_token[:, :], bank[2][:, 0:NT])
                link(v.tensor_copy(prob_sum[:, :], bank[2][:, NT:2 * NT]))
                v.tensor_tensor(slot_prob[:, :], prob_sum[:, :], bank[2][:, 2 * NT:3 * NT], ALU.add)

        tok = [sb(f"tok{i}", [P, KD, T]) for i in range(2)]
        tok_loaded = [sem(f"tok_loaded{i}") for i in range(2)]

        def load_tokens(eng, b, i):
            eng.dma_start(tok[i][:, :, :], hidden[bass.ds(b * D, D), :].rearrange("(k p) t -> p k t", p=P))\
                .then_inc(tok_loaded[i], 16)

        experts = ExitStack()
        ctx.enter_context(experts)
        with experts:
            def eb(name, shape, dt=F32):
                return [experts.enter_context(nc.sbuf_tensor(f"{name}{i}", shape, dt)) for i in range(2)]

            def esem(name):
                return experts.enter_context(nc.semaphore(name))

            row_no = eb("row_no", [P, 1], I32)
            row_prob = eb("row_prob", [P, 1])
            rows_in = eb("rows_in", [P, T])
            rows_scaled = eb("rows_scaled", [P, T])
            rows_T = eb("rows_T", [P, KT, P])
            gated = eb("gated", [P, I])
            act_h = eb("act_h", [P, I])
            act_hT = eb("act_hT", [P, KI, P])
            rows_out = eb("rows_out", [P, T])
            inT_bank, gu_bank, hT_bank, out_bank = bank[0:2], bank[2:4], bank[4:6], bank[6:8]

            gathered = [esem(f"gathered{i}") for i in range(2)]
            row_no_ready = esem("row_no_ready")
            scaled = esem("scaled")
            in_turned = esem("in_turned")
            in_copied = esem("in_copied")
            gu_done = esem("gu_done")
            silu_done = esem("silu_done")
            h_done = esem("h_done")
            h_turned = esem("h_turned")
            h_copied = esem("h_copied")
            down_done = esem("down_done")
            out_copied = esem("out_copied")
            stored = [esem(f"stored{i}") for i in range(2)]
            block3 = experts.enter_context(nc.Block())

            def tiles(eng, step):
                for n in range(4):
                    step(n, n % 2)
                with eng.Fori(2, NT // 2 - 1) as n:
                    for i in range(2):
                        step(2 * n + i, i)
                for n in range(NT - 2, NT + 1):
                    step(n, n % 2)

            def first(n):
                return isinstance(n, int) and n < 2

            def exists(n):
                return not isinstance(n, int) or 0 <= n < NT

            @block3.gpsimd
            def _(pool):
                def step(n, i):
                    if not exists(n):
                        return
                    if not first(n):
                        pool.wait_ge(scaled, n - 1)
                    nc.gpsimd.tensor_copy(row_prob[i][:, :], slot_prob[:, bass.ds(n, 1)])
                    nc.gpsimd.tensor_copy(row_no[i][:, :], slot_token[:, bass.ds(n, 1)]).then_inc(row_no_ready, 1)
                    pool.wait_ge(row_no_ready, n + 1)
                    pool.sem_inc(pool_waits_passed, 1)
                    nc.gpsimd.indirect_dma_start(rows_in[i][:, :], None, hidden[:, :],
                                                 bass.IndirectOffsetOnAxis(ap=row_no[i][:, 0:1], axis=0))\
                        .then_inc(gathered[i], 16)
                tiles(pool, step)

            @block3.vector
            def _(dve):
                def scale_rows(n, i):
                    dve.wait_ge(gathered[i], 8 * (n - i) + 16)
                    if not first(n):
                        dve.wait_ge(in_turned, n - 1)
                    nc.vector.tensor_scalar(rows_scaled[i][:, :], rows_in[i][:, :], row_prob[i][:, 0:1], None, ALU.mult)\
                        .then_inc(scaled, 1)

                def combine(n, i):
                    dve.wait_ge(silu_done, n + 1)
                    if not first(n):
                        dve.wait_ge(h_turned, n - 1)
                    nc.vector.tensor_tensor(act_h[i][:, :], gated[i][:, :], gu_bank[i][:, I:F2], ALU.mult)\
                        .then_inc(h_done, 1)

                def copy_h(n, i):
                    dve.wait_ge(h_turned, n + 1)
                    if not first(n):
                        dve.wait_ge(down_done, n - 1)
                    nc.vector.tensor_copy(act_hT[i][:, :, :],
                                          hT_bank[i][:, 0:I].rearrange("p (k c) -> p k c", k=KI)).then_inc(h_copied, 1)

                def step(n, i):
                    if exists(n - 1):
                        copy_h(n - 1, 1 - i)
                    if exists(n):
                        combine(n, i)
                    if exists(n + 2):
                        scale_rows(n + 2, i)
                for n in range(2):
                    scale_rows(n, n)
                tiles(dve, step)

            @block3.scalar
            def _(act):
                def copy_in(n, i):
                    act.wait_ge(in_turned, n + 1)
                    if not first(n):
                        act.wait_ge(gu_done, n - 1)
                    nc.scalar.activation(rows_T[i][:, :, :], inT_bank[i][:, :].rearrange("p (k c) -> p k c", k=KT),
                                         ACT.Copy).then_inc(in_copied, 1)

                def silu(n, i):
                    act.wait_ge(gu_done, n + 1)
                    if not first(n):
                        act.wait_ge(h_done, n - 1)
                    nc.scalar.activation(gated[i][:, :], gu_bank[i][:, 0:I], ACT.Silu).then_inc(silu_done, 1)

                def copy_out(n, i):
                    act.wait_ge(down_done, n + 1)
                    if not first(n):
                        act.wait_ge(stored[i], 8 * (n - i))
                    nc.scalar.activation(rows_out[i][:, :], out_bank[i][:, :], ACT.Copy).then_inc(out_copied, 1)

                def step(n, i):
                    if exists(n):
                        silu(n, i)
                    if exists(n + 1):
                        copy_in(n + 1, 1 - i)
                    if exists(n - 1):
                        copy_out(n - 1, 1 - i)
                copy_in(0, 0)
                tiles(act, step)

            @block3.sync
            def _(sp):
                def step(n, i):
                    if isinstance(n, int) and n in (2, 3):
                        load_tokens(sp, n - 2, i)
                    if exists(n - 1):
                        sp.wait_ge(out_copied, n)
                        sp.sem_inc(sp_waits_passed, 1)
                        sp.dma_start(expert_rows[bass.ds((n - 1) * P, P), :], rows_out[1 - i][:, :])\
                            .then_inc(stored[1 - i], 16)
                tiles(sp, step)
                for i in range(2):
                    sp.wait_ge(stored[i], 8 * NT)

            @block3.tensor
            def _(pe):
                pe.wait_ge(experts_loaded, 2 * E * 16)

                def expert(n):
                    return pe.value_load(tile_expert[0:1, bass.ds(n, 1)], min_val=0, max_val=E - 1)

                def turn_in(n, i):
                    pe.wait_ge(scaled, n + 1)
                    if not first(n):
                        pe.wait_ge(in_copied, n - 1)
                    for k in range(KT):
                        last = nc.tensor.transpose(inT_bank[i][:, k * P:(k + 1) * P],
                                                   rows_scaled[i][:, k * P:(k + 1) * P], ident[:, :])
                    last.then_inc(in_turned, 1)

                def gate_up(n, i, e):
                    pe.wait_ge(in_copied, n + 1)
                    if not first(n):
                        pe.wait_ge(h_done, n - 1)
                    for k in range(KT):
                        if k == KT // 2 and exists(n - 1):
                            turn_h(n - 1, 1 - i)
                        w = gate_up_sb[:, bass.ds(e * KT + k, 1), :].rearrange("p o f -> p (o f)")
                        last = nc.tensor.matmul(gu_bank[i][:, :], rows_T[i][:, k, :], w,
                                                start=(k == 0), stop=(k == KT - 1))
                    last.then_inc(gu_done, 1)

                def turn_h(n, i):
                    pe.wait_ge(h_done, n + 1)
                    if not first(n):
                        pe.wait_ge(h_copied, n - 1)
                    for k in range(KI):
                        last = nc.tensor.transpose(hT_bank[i][:, k * P:(k + 1) * P],
                                                   act_h[i][:, k * P:(k + 1) * P], ident[:, :])
                    last.then_inc(h_turned, 1)

                def down(n, i, e):
                    pe.wait_ge(h_copied, n + 1)
                    if not first(n):
                        pe.wait_ge(out_copied, n - 1)
                    for k in range(KI):
                        w = down_sb[:, bass.ds(e * KI + k, 1), :].rearrange("p o f -> p (o f)")
                        last = nc.tensor.matmul(out_bank[i][:, :], act_hT[i][:, k, :], w,
                                                start=(k == 0), stop=(k == KI - 1))
                    last.then_inc(down_done, 1)

                def step(n, i):
                    if exists(n):
                        gate_up(n, i, expert(n))
                    elif exists(n - 1):
                        turn_h(n - 1, 1 - i)
                    if exists(n + 1):
                        turn_in(n + 1, 1 - i)
                    if exists(n - 1):
                        down(n - 1, 1 - i, expert(n - 1))
                turn_in(0, 0)
                tiles(pe, step)

        shared = ExitStack()
        ctx.enter_context(shared)
        with shared:
            def fb(name, shape, dt=F32):
                return [shared.enter_context(nc.sbuf_tensor(f"{name}{i}", shape, dt)) for i in range(2)]

            def fsem(name):
                return shared.enter_context(nc.semaphore(name))

            x_in = fb("x_in", [P, KD, T])
            tokT_hi = fb("tokT_hi", [P, KT, D], F32R)
            tokT_lo = fb("tokT_lo", [P, KT, D], F32R)
            sgate = fb("sgate", [P, KI, D])
            sh = fb("sh", [P, KI, D])
            sh_hi = fb("sh_hi", [P, KI, D], F32R)
            sh_lo = fb("sh_lo", [P, KI, D], F32R)
            slot_no = [[fb(f"slot_no{c}_{i}_", [P, 1], I32) for i in range(2)] for c in range(2)]
            expert_row = [[fb(f"expert_row{c}_{i}_", [P, T]) for i in range(2)] for c in range(2)]
            total = fb("total", [P, T])
            gate_bank, up_bank, sum_bank = (bank[2], bank[4]), (bank[3], bank[5]), bank[6:8]

            x_in_loaded = [fsem(f"x_in_loaded{i}") for i in range(2)]
            tok_turned = fsem("tok_turned")
            tokT_hi_ready = fsem("tokT_hi_ready")
            tokT_lo_ready = fsem("tokT_lo_ready")
            up_done = fsem("up_done")
            sgate_done = fsem("sgate_done")
            sh_done = fsem("sh_done")
            sh_hi_ready = fsem("sh_hi_ready")
            sh_lo_ready = fsem("sh_lo_ready")
            shared_done = fsem("shared_done")
            slot_no_ready = fsem("slot_no_ready")
            row_gathered = [[fsem(f"row_gathered{i}_{h}") for h in range(KD)] for i in range(2)]
            row_sum_ready = fsem("row_sum_ready")
            x_added = fsem("x_added")
            total_ready = fsem("total_ready")
            out_stored = [fsem(f"out_stored{i}") for i in range(2)]
            block4 = shared.enter_context(nc.Block())

            def row_steps(eng, step):
                for b in range(4):
                    step(b, b % 2)
                with eng.Fori(2, B // 2 - 1) as n:
                    for i in range(2):
                        step(2 * n + i, i)
                for b in range(B - 2, B + 1):
                    step(b, b % 2)

            def first_rows(b, n=2):
                return isinstance(b, int) and b < n

            def is_row(b):
                return not isinstance(b, int) or 0 <= b < B

            out_rows = out.rearrange("b d t -> (b d) t")

            @block4.sync
            def _(sp):
                def load(b, i):
                    if not first_rows(b):
                        sp.wait_ge(tok_turned, 2 * (b - 1))
                        sp.sem_inc(sp_waits_passed, 1)
                    load_tokens(sp, b, i)

                def load_x(b, i):
                    if not first_rows(b):
                        sp.wait_ge(x_added, 2 * (b - 1))
                        sp.sem_inc(sp_waits_passed, 1)
                    sp.dma_start(x_in[i][:, :, :], x[bass.ds(b, 1)].rearrange("o (k p) t -> p (o k) t", p=P))\
                        .then_inc(x_in_loaded[i], 16)

                def store(b):
                    for h in range(KD):
                        sp.wait_ge(total_ready, 2 * b + h + 1)
                        sp.sem_inc(sp_waits_passed, 1)
                        sp.dma_start(out_rows[bass.ds((2 * b + h) * P, P), :], total[h][:, :])\
                            .then_inc(out_stored[h], 16)

                def step(b, i):
                    if is_row(b):
                        load_x(b, i)
                    if is_row(b + 2):
                        load(b + 2, i)
                    if is_row(b - 1):
                        store(b - 1)
                row_steps(sp, step)
                for h in range(KD):
                    sp.wait_ge(out_stored[h], 16 * B)

            @block4.scalar
            def _(act):
                def copy_tokens(b, i):
                    for h in range(2):
                        act.wait_ge(tok_turned, 2 * b + h + 1)
                        if h == 0 and not first_rows(b):
                            act.wait_ge(up_done, b - 1)
                        nc.scalar.activation(tokT_hi[i][:, 2 * h:2 * h + 2, :],
                                             bank[h][:, :].rearrange("p (k c) -> p k c", k=2), ACT.Copy)\
                            .then_inc(tokT_hi_ready, 1)

                def silu(b, i):
                    act.wait_ge(up_done, b + 1)
                    if not first_rows(b):
                        act.wait_ge(sh_done, b - 1)
                    nc.scalar.activation(sgate[i][:, :, :], gate_bank[i][:, :].rearrange("p (k c) -> p k c", k=KI),
                                         ACT.Silu).then_inc(sgate_done, 1)

                def upper_sh(b, i):
                    act.wait_ge(sh_done, b + 1)
                    if not first_rows(b):
                        act.wait_ge(shared_done, 2 * (b - 1))
                    nc.scalar.activation(sh_hi[i][:, :, :], sh[i][:, :, :], ACT.Copy).then_inc(sh_hi_ready, 1)

                def step(b, i):
                    if is_row(b):
                        silu(b, i)
                    if is_row(b + 1):
                        copy_tokens(b + 1, 1 - i)
                    if is_row(b):
                        upper_sh(b, i)
                copy_tokens(0, 0)
                row_steps(act, step)

            @block4.tensor
            def _(pe):
                def products(dst, pairs):
                    for n, (a, b) in enumerate(pairs):
                        last = nc.tensor.matmul(dst, a, b, start=(n == 0), stop=(n == len(pairs) - 1))
                    return last

                def turn_tokens(b, i):
                    pe.wait_ge(tok_loaded[i], 8 * (b - i) + 16)
                    for h in range(2):
                        if not first_rows(b, 1):
                            pe.wait_ge(tokT_lo_ready, 2 * b - 1 + h)
                        for k in range(2):
                            for m in range(KD):
                                c = k * D + m * P
                                last = nc.tensor.transpose(bank[h][:, c:c + P],
                                                           tok[i][:, m, (2 * h + k) * P:(2 * h + k + 1) * P], ident[:, :])
                        last.then_inc(tok_turned, 1)

                def gate_up(b, i):
                    pe.wait_ge(tokT_lo_ready, 2 * b + 2)
                    if not first_rows(b):
                        pe.wait_ge(sh_done, b - 1)
                    for hi, lo, dst in zip(shared_in_hi, shared_in_lo, (gate_bank[i], up_bank[i])):
                        for m in range(KI):
                            last = products(dst[:, m * D:(m + 1) * D],
                                            [(w[:, k, m * P:(m + 1) * P], t[i][:, k, :])
                                             for k in range(KT) for w, t in ((hi, tokT_hi), (hi, tokT_lo), (lo, tokT_hi))])
                    last.then_inc(up_done, 1)

                def down(b, i):
                    pe.wait_ge(sh_lo_ready, b + 1)
                    for h in range(KD):
                        if not first_rows(b, 1):
                            pe.wait_ge(total_ready, 2 * b - 1 + h)
                        products(sum_bank[h][:, :],
                                 [(s[i][:, k, h * P:(h + 1) * P], w[:, k, :]) for k in range(KI)
                                  for s, w in ((sh_hi, shared_out_hi), (sh_hi, shared_out_lo), (sh_lo, shared_out_hi))])\
                            .then_inc(shared_done, 1)

                def step(b, i):
                    if is_row(b):
                        gate_up(b, i)
                    if is_row(b + 1):
                        turn_tokens(b + 1, 1 - i)
                    if is_row(b - 1):
                        down(b - 1, 1 - i)
                turn_tokens(0, 0)
                row_steps(pe, step)

            @block4.gpsimd
            def _(pool):
                def step(b, i):
                    if not is_row(b):
                        return
                    for h in range(KD):
                        n = 2 * b + h
                        if not first_rows(b):
                            pool.wait_ge(total_ready, n - 3)
                        for c in range(2):
                            nc.gpsimd.tensor_copy(slot_no[c][i][h][:, :], token_slot[:, c, bass.ds(n, 1)])\
                                .then_inc(slot_no_ready, 1)
                        pool.wait_ge(slot_no_ready, 2 * n + 2)
                        pool.sem_inc(pool_waits_passed, 1)
                        for c in range(2):
                            nc.gpsimd.indirect_dma_start(expert_row[c][i][h][:, :], None, expert_rows[:, :],
                                                         bass.IndirectOffsetOnAxis(ap=slot_no[c][i][h][:, 0:1], axis=0))\
                                .then_inc(row_gathered[i][h], 16)
                row_steps(pool, step)

            @block4.vector
            def _(dve):
                def lower_tokens(b, i):
                    for h in range(2):
                        dve.wait_ge(tokT_hi_ready, 2 * b + h + 1)
                        if h == 0 and not first_rows(b):
                            dve.wait_ge(up_done, b - 1)
                        part = tokT_hi[i][:, 2 * h:2 * h + 2, :]
                        nc.vector.tensor_tensor(tokT_lo[i][:, 2 * h:2 * h + 2, :],
                                                bank[h][:, :].rearrange("p (k c) -> p k c", k=2),
                                                part.bitcast(F32), ALU.subtract).then_inc(tokT_lo_ready, 1)

                def lower_sh(b, i):
                    dve.wait_ge(sh_hi_ready, b + 1)
                    if not first_rows(b):
                        dve.wait_ge(shared_done, 2 * (b - 1))
                    nc.vector.tensor_tensor(sh_lo[i][:, :, :], sh[i][:, :, :], sh_hi[i][:, :, :].bitcast(F32),
                                            ALU.subtract).then_inc(sh_lo_ready, 1)

                def combine(b, i):
                    dve.wait_ge(sgate_done, b + 1)
                    if not first_rows(b):
                        dve.wait_ge(sh_lo_ready, b - 1)
                    nc.vector.tensor_tensor(sh[i][:, :, :], sgate[i][:, :, :],
                                            up_bank[i][:, :].rearrange("p (k c) -> p k c", k=KI), ALU.mult)\
                        .then_inc(sh_done, 1)

                def add_up(b, i):
                    for h in range(KD):
                        rows = [expert_row[c][i][h] for c in range(2)]
                        dve.wait_ge(row_gathered[i][h], 16 * (b - i) + 32)
                        nc.vector.tensor_tensor(rows[0][:, :], rows[0][:, :], rows[1][:, :],
                                                ALU.add).then_inc(row_sum_ready, 1)
                    dve.wait_ge(x_in_loaded[i], 8 * (b - i) + 16)
                    for h in range(KD):
                        rows = [expert_row[c][i][h] for c in range(2)]
                        dve.wait_ge(row_sum_ready, 2 * b + h + 1)
                        nc.vector.tensor_tensor(rows[0][:, :], rows[0][:, :], x_in[i][:, h, :], ALU.add)\
                            .then_inc(x_added, 1)
                    for h in range(KD):
                        rows = [expert_row[c][i][h] for c in range(2)]
                        n = 2 * b + h
                        dve.wait_ge(x_added, n + 1)
                        dve.wait_ge(shared_done, n + 1)
                        if not first_rows(b, 1):
                            dve.wait_ge(out_stored[h], 16 * b)
                        nc.vector.tensor_tensor(total[h][:, :], sum_bank[h][:, :], rows[0][:, :], ALU.add)\
                            .then_inc(total_ready, 1)

                def step(b, i):
                    if is_row(b):
                        combine(b, i)
                    if is_row(b + 1):
                        lower_tokens(b + 1, 1 - i)
                    if is_row(b):
                        lower_sh(b, i)
                    if is_row(b - 1):
                        add_up(b - 1, 1 - i)
                lower_tokens(0, 0)
                row_steps(dve, step)



_INS = ["x", "cond_2048", "L0_cond_Wq", "L0_cond_Wo", "L0_ffn_router_w", "L0_ffn_gate_up_w", "L0_ffn_down_w",
        "L0_ffn_shared_gate_w", "L0_ffn_shared_up_w", "L0_ffn_shared_down_w"]


def kernel(**inputs):
    import numpy as np
    import concourse.bacc as bacc
    from concourse.bass_utils import run_bass_kernel_spmd

    nc = bacc.Bacc("TRN2", target_bir_lowering=False, num_devices=1)
    arrays, args = {}, []
    for name in _INS:
        a = np.ascontiguousarray(inputs[name])
        arrays[f"in_{name}"] = a
        args.append(nc.dram_tensor(f"in_{name}", a.shape, mybir.dt.from_np(a.dtype), kind="ExternalInput").ap())
    shape = inputs["x"].shape
    args.append(nc.dram_tensor("out_0", shape, F32, kind="ExternalOutput").ap())
    build(nc, *args)
    r = run_bass_kernel_spmd(nc, [arrays], core_ids=[0])
    return r.results[0]["out_0"]
```
